# Optimizing a Trainium2 kernel written in Bass

```python
import numpy as np
import jax
import jax.numpy as jnp

def _softmax(x, axis=-1):
    return jax.nn.softmax(x, axis=axis)

def _gelu(x):
    return jax.nn.gelu(x, approximate=True)

def _silu(x):
    return jax.nn.silu(x)

def _sigmoid(x):
    return jax.nn.sigmoid(x)

def _layernorm(x, axis=-1, eps=1e-05):
    m = jnp.mean(x, axis=axis, keepdims=True)
    v = jnp.var(x, axis=axis, keepdims=True)
    return (x - m) / jnp.sqrt(v + eps)

def _scatter_add(tgt, idx, src, axis=0):
    return tgt.at[idx].add(src)

def _segment_sum(src, seg, n):
    return jax.ops.segment_sum(src, seg, n)
kernel_name = 'mk_dlrm_tower_d1_rec_r8_df1f7a'

def setup_inputs(seed: int=0):
    np.random.seed(seed)
    _w = jnp.asarray

    def _rec_inputs():
        import jax
        import jax.numpy as jnp
        _tk = jax.random.key(seed)
        ids = jnp.stack([jax.random.randint(jax.random.fold_in(_tk, 200 + f), (2048,), 0, v, jnp.int32) for f, v in enumerate([12500, 1250, 125000, 1250, 1000, 12500, 1000, 12500, 125000, 1000, 1250, 1000, 1250, 1000, 1000, 12500, 125000, 12500, 12500, 1000, 1000, 12500, 1000, 1000, 1000, 12500])], axis=1)
        tbl_0 = 0.05 * jax.random.normal(jax.random.fold_in(_tk, 500 + 0), (12500, 64), jnp.float32)
        tbl_1 = 0.05 * jax.random.normal(jax.random.fold_in(_tk, 500 + 1), (1250, 64), jnp.float32)
        tbl_2 = 0.05 * jax.random.normal(jax.random.fold_in(_tk, 500 + 2), (125000, 64), jnp.float32)
        tbl_3 = 0.05 * jax.random.normal(jax.random.fold_in(_tk, 500 + 3), (1250, 64), jnp.float32)
        tbl_4 = 0.05 * jax.random.normal(jax.random.fold_in(_tk, 500 + 4), (1000, 64), jnp.float32)
        tbl_5 = 0.05 * jax.random.normal(jax.random.fold_in(_tk, 500 + 5), (12500, 64), jnp.float32)
        tbl_6 = 0.05 * jax.random.normal(jax.random.fold_in(_tk, 500 + 6), (1000, 64), jnp.float32)
        tbl_7 = 0.05 * jax.random.normal(jax.random.fold_in(_tk, 500 + 7), (12500, 64), jnp.float32)
        tbl_8 = 0.05 * jax.random.normal(jax.random.fold_in(_tk, 500 + 8), (125000, 64), jnp.float32)
        tbl_9 = 0.05 * jax.random.normal(jax.random.fold_in(_tk, 500 + 9), (1000, 64), jnp.float32)
        tbl_10 = 0.05 * jax.random.normal(jax.random.fold_in(_tk, 500 + 10), (1250, 64), jnp.float32)
        tbl_11 = 0.05 * jax.random.normal(jax.random.fold_in(_tk, 500 + 11), (1000, 64), jnp.float32)
        tbl_12 = 0.05 * jax.random.normal(jax.random.fold_in(_tk, 500 + 12), (1250, 64), jnp.float32)
        tbl_13 = 0.05 * jax.random.normal(jax.random.fold_in(_tk, 500 + 13), (1000, 64), jnp.float32)
        tbl_14 = 0.05 * jax.random.normal(jax.random.fold_in(_tk, 500 + 14), (1000, 64), jnp.float32)
        tbl_15 = 0.05 * jax.random.normal(jax.random.fold_in(_tk, 500 + 15), (12500, 64), jnp.float32)
        tbl_16 = 0.05 * jax.random.normal(jax.random.fold_in(_tk, 500 + 16), (125000, 64), jnp.float32)
        tbl_17 = 0.05 * jax.random.normal(jax.random.fold_in(_tk, 500 + 17), (12500, 64), jnp.float32)
        tbl_18 = 0.05 * jax.random.normal(jax.random.fold_in(_tk, 500 + 18), (12500, 64), jnp.float32)
        tbl_19 = 0.05 * jax.random.normal(jax.random.fold_in(_tk, 500 + 19), (1000, 64), jnp.float32)
        tbl_20 = 0.05 * jax.random.normal(jax.random.fold_in(_tk, 500 + 20), (1000, 64), jnp.float32)
        tbl_21 = 0.05 * jax.random.normal(jax.random.fold_in(_tk, 500 + 21), (12500, 64), jnp.float32)
        tbl_22 = 0.05 * jax.random.normal(jax.random.fold_in(_tk, 500 + 22), (1000, 64), jnp.float32)
        tbl_23 = 0.05 * jax.random.normal(jax.random.fold_in(_tk, 500 + 23), (1000, 64), jnp.float32)
        tbl_24 = 0.05 * jax.random.normal(jax.random.fold_in(_tk, 500 + 24), (1000, 64), jnp.float32)
        tbl_25 = 0.05 * jax.random.normal(jax.random.fold_in(_tk, 500 + 25), (12500, 64), jnp.float32)
        _rk = jax.random.fold_in(_tk, 7)
        r_dense_t = 7.22013e-05 + 1.00017 * jax.random.normal(jax.random.fold_in(_rk, 101), (2048, 256), jnp.float32)
        W_top1 = 0.0360844 * jax.random.normal(jax.random.fold_in(_tk, 801), (768, 512), jnp.float32)
        W_top2 = 0.0441942 * jax.random.normal(jax.random.fold_in(_tk, 802), (512, 256), jnp.float32)
        W_top3 = 0.0625 * jax.random.normal(jax.random.fold_in(_tk, 803), (256, 1), jnp.float32)
        b_top1 = jnp.zeros((512,), jnp.float32)
        b_top2 = jnp.zeros((256,), jnp.float32)
        return (r_dense_t, ids, tbl_0, tbl_1, tbl_2, tbl_3, tbl_4, tbl_5, tbl_6, tbl_7, tbl_8, tbl_9, tbl_10, tbl_11, tbl_12, tbl_13, tbl_14, tbl_15, tbl_16, tbl_17, tbl_18, tbl_19, tbl_20, tbl_21, tbl_22, tbl_23, tbl_24, tbl_25, W_top1, b_top1, W_top2, b_top2, W_top3)
    r_dense_t, ids, tbl_0, tbl_1, tbl_2, tbl_3, tbl_4, tbl_5, tbl_6, tbl_7, tbl_8, tbl_9, tbl_10, tbl_11, tbl_12, tbl_13, tbl_14, tbl_15, tbl_16, tbl_17, tbl_18, tbl_19, tbl_20, tbl_21, tbl_22, tbl_23, tbl_24, tbl_25, W_top1, b_top1, W_top2, b_top2, W_top3 = _rec_inputs()

    def _L0_rec_setup():
        import jax, jax.numpy as jnp
        import numpy as np
        EPS = 1e-05
        NI = 33
        TRIL_I, TRIL_J = np.tril_indices(NI, k=-1)

        def layer_norm(x, g, b):
            m = jnp.mean(x, axis=-1, keepdims=True)
            v = jnp.mean(jnp.square(x - m), axis=-1, keepdims=True)
            return (x - m) * jax.lax.rsqrt(v + EPS) * g + b
        key = jax.random.key(seed)
        ks = jax.random.split(key, 8)
        B, D_DENSE, N_SP, D_SP = (4096, 256, 26, 64)
        E, PROJ, MAXD, NFLAT = (128, 32, 512, 528)
        dense_t = jax.random.normal(ks[0], (B, D_DENSE), dtype=jnp.float32)
        sparse_t = jax.random.normal(ks[1], (B, N_SP, D_SP), dtype=jnp.float32)
        Wd = jax.random.normal(ks[2], (E, D_DENSE), dtype=jnp.float32) / np.sqrt(D_DENSE)
        Ws = jax.random.normal(ks[3], (E, D_SP), dtype=jnp.float32) / np.sqrt(D_SP)
        Wsi = jax.random.normal(ks[4], (PROJ, N_SP), dtype=jnp.float32) / np.sqrt(N_SP)
        Wl = jax.random.normal(ks[5], (MAXD, NFLAT), dtype=jnp.float32) / np.sqrt(NFLAT)
        gd = jnp.ones((E,), jnp.float32)
        bd = jnp.zeros((E,), jnp.float32)
        gs = jnp.ones((E,), jnp.float32)
        bs = jnp.zeros((E,), jnp.float32)
        gsi = jnp.ones((PROJ,), jnp.float32)
        bsi = jnp.zeros((PROJ,), jnp.float32)
        gl = jnp.ones((MAXD,), jnp.float32)
        bl = jnp.zeros((MAXD,), jnp.float32)
        return {'dense_t': dense_t, 'sparse_t': sparse_t, 'Wd': Wd, 'gd': gd, 'bd': bd, 'Ws': Ws, 'gs': gs, 'bs': bs, 'Wsi': Wsi, 'gsi': gsi, 'bsi': bsi, 'Wl': Wl, 'gl': gl, 'bl': bl, 'dims_in_use': 384}
    _L0_rec_all = _L0_rec_setup()
    _L0_rec_in = {k: v for k, v in _L0_rec_all.items() if k in ('Wd', 'gd', 'bd', 'Ws', 'gs', 'bs', 'Wsi', 'gsi', 'bsi', 'Wl', 'gl', 'bl')}
    del _L0_rec_all
    return {'r_dense_t': r_dense_t, 'ids': ids, 'tbl_0': tbl_0, 'tbl_1': tbl_1, 'tbl_2': tbl_2, 'tbl_3': tbl_3, 'tbl_4': tbl_4, 'tbl_5': tbl_5, 'tbl_6': tbl_6, 'tbl_7': tbl_7, 'tbl_8': tbl_8, 'tbl_9': tbl_9, 'tbl_10': tbl_10, 'tbl_11': tbl_11, 'tbl_12': tbl_12, 'tbl_13': tbl_13, 'tbl_14': tbl_14, 'tbl_15': tbl_15, 'tbl_16': tbl_16, 'tbl_17': tbl_17, 'tbl_18': tbl_18, 'tbl_19': tbl_19, 'tbl_20': tbl_20, 'tbl_21': tbl_21, 'tbl_22': tbl_22, 'tbl_23': tbl_23, 'tbl_24': tbl_24, 'tbl_25': tbl_25, 'W_top1': W_top1, 'b_top1': b_top1, 'W_top2': W_top2, 'b_top2': b_top2, 'W_top3': W_top3, 'L0_rec_Wd': _L0_rec_in['Wd'], 'L0_rec_gd': _L0_rec_in['gd'], 'L0_rec_bd': _L0_rec_in['bd'], 'L0_rec_Ws': _L0_rec_in['Ws'], 'L0_rec_gs': _L0_rec_in['gs'], 'L0_rec_bs': _L0_rec_in['bs'], 'L0_rec_Wsi': _L0_rec_in['Wsi'], 'L0_rec_gsi': _L0_rec_in['gsi'], 'L0_rec_bsi': _L0_rec_in['bsi'], 'L0_rec_Wl': _L0_rec_in['Wl'], 'L0_rec_gl': _L0_rec_in['gl'], 'L0_rec_bl': _L0_rec_in['bl']}

def reference(r_dense_t, ids, tbl_0, tbl_1, tbl_2, tbl_3, tbl_4, tbl_5, tbl_6, tbl_7, tbl_8, tbl_9, tbl_10, tbl_11, tbl_12, tbl_13, tbl_14, tbl_15, tbl_16, tbl_17, tbl_18, tbl_19, tbl_20, tbl_21, tbl_22, tbl_23, tbl_24, tbl_25, W_top1, b_top1, W_top2, b_top2, W_top3, L0_rec_Wd, L0_rec_gd, L0_rec_bd, L0_rec_Ws, L0_rec_gs, L0_rec_bs, L0_rec_Wsi, L0_rec_gsi, L0_rec_bsi, L0_rec_Wl, L0_rec_gl, L0_rec_bl):
    import jax
    import jax.numpy as jnp

    def _L0_rec_ref(dense_t, sparse_t, Wd, gd, bd, Ws, gs, bs, Wsi, gsi, bsi, Wl, gl, bl, dims_in_use):
        import jax, jax.numpy as jnp
        import numpy as np
        EPS = 1e-05
        NI = 33
        TRIL_I, TRIL_J = np.tril_indices(NI, k=-1)

        def layer_norm(x, g, b):
            m = jnp.mean(x, axis=-1, keepdims=True)
            v = jnp.mean(jnp.square(x - m), axis=-1, keepdims=True)
            return (x - m) * jax.lax.rsqrt(v + EPS) * g + b
        x = layer_norm(dense_t @ Wd.T, gd, bd)
        y = layer_norm(jnp.einsum('bnd,ed->bne', sparse_t, Ws), gs, bs)
        y = jnp.einsum('bne,pn->bep', y, Wsi)
        y = layer_norm(y, gsi, bsi)
        y = jnp.swapaxes(y, 1, 2)
        T = jnp.concatenate([x[:, None, :], y], axis=1)
        Z = jnp.einsum('bnd,bmd->bnm', T, T)
        Zflat = Z[:, TRIL_I, TRIL_J]
        out = layer_norm(Zflat @ Wl.T, gl, bl)
        maxd = out.shape[-1]
        mask = (jnp.arange(maxd) < dims_in_use).astype(out.dtype)
        return out * mask
    e = jnp.stack([tbl_0[ids[:, 0]], tbl_1[ids[:, 1]], tbl_2[ids[:, 2]], tbl_3[ids[:, 3]], tbl_4[ids[:, 4]], tbl_5[ids[:, 5]], tbl_6[ids[:, 6]], tbl_7[ids[:, 7]], tbl_8[ids[:, 8]], tbl_9[ids[:, 9]], tbl_10[ids[:, 10]], tbl_11[ids[:, 11]], tbl_12[ids[:, 12]], tbl_13[ids[:, 13]], tbl_14[ids[:, 14]], tbl_15[ids[:, 15]], tbl_16[ids[:, 16]], tbl_17[ids[:, 17]], tbl_18[ids[:, 18]], tbl_19[ids[:, 19]], tbl_20[ids[:, 20]], tbl_21[ids[:, 21]], tbl_22[ids[:, 22]], tbl_23[ids[:, 23]], tbl_24[ids[:, 24]], tbl_25[ids[:, 25]]], axis=1)
    z = _L0_rec_ref(r_dense_t, e, L0_rec_Wd, L0_rec_gd, L0_rec_bd, L0_rec_Ws, L0_rec_gs, L0_rec_bs, L0_rec_Wsi, L0_rec_gsi, L0_rec_bsi, L0_rec_Wl, L0_rec_gl, L0_rec_bl, 384)
    z = z.reshape(z.shape[0], -1)
    h = jnp.concatenate([z, r_dense_t], axis=1)
    h = jnp.maximum(h @ W_top1 + b_top1, 0.0)
    h = jnp.maximum(h @ W_top2 + b_top2, 0.0)
    y = h @ W_top3
    return y

_drawn_inputs = setup_inputs


def setup_inputs(seed=0):
    import zlib

    import numpy as np

    out = dict(_drawn_inputs(seed))
    spreads = {'b_top1': (0.0, 0.1),
     'b_top2': (0.0, 0.1),
     'L0_rec_gd': (1.0, 0.6),
     'L0_rec_bd': (0.0, 0.8),
     'L0_rec_gs': (1.0, 0.6),
     'L0_rec_bs': (0.0, 0.1),
     'L0_rec_gsi': (1.0, 0.2),
     'L0_rec_bsi': (0.0, 0.1),
     'L0_rec_gl': (1.0, 0.2),
     'L0_rec_bl': (0.0, 0.1)}
    factors = {}
    for name, (base, spread) in spreads.items():
        noise = np.random.default_rng([zlib.crc32(name.encode()), seed]).standard_normal(out[name].shape)
        drawn = base * np.exp(spread * noise) if base else spread * noise
        out[name] = jnp.asarray(drawn.astype(out[name].dtype))
    for name, factor in factors.items():
        out[name] = (out[name] * factor).astype(out[name].dtype)
    return out
```

```python
import numpy as np
import concourse.bass as bass
from concourse import mybir
from contextlib import ExitStack

VOCABS = [12500, 1250, 125000, 1250, 1000, 12500, 1000, 12500, 125000, 1000, 1250, 1000, 1250,
          1000, 1000, 12500, 125000, 12500, 12500, 1000, 1000, 12500, 1000, 1000, 1000, 12500]
B, NS, D, E, P, KD = 2048, 26, 64, 128, 32, 256
OUT_LN, DIMS, H1, H2 = 512, 384, 512, 256
TB = 128
NT = B // TB
J = 4
G = TB // J
CH = 4
GC = G // CH
JN = J * NS
JP = J * P
W34 = P + 2
TW = J * W34
NPAIR = NS // 2
EPS = 1e-5
N_EXT = P + 2
K4 = N_EXT + P // 2


def pair_blocks():
    blocks = [[(p, q) for p in range(16, 24) for q in range(16)],
              [(p, q) for p in range(24, 32) for q in range(16)],
              [(16 * s + 8 + r, 16 * s + c) for s in range(2) for r in range(8) for c in range(8)],
              [(8 * s + 4 + r, 8 * s + c) for s in range(4) for r in range(4) for c in range(4)]
              + [(4 * s + 2 + r, 4 * s + c) for s in range(8) for r in range(2) for c in range(2)]
              + [(2 * s + 1, 2 * s) for s in range(16)] + [(p, -1) for p in range(16)],
              [None] * N_EXT + [(p, -1) for p in range(16, 32)]]
    return blocks


def build(nc, ids, tables, dT, WdT, gd, bd, Ws, gs, bs, WsiT, gsi, bsi, WlT, glc, blc,
          W1, b1c, W2, b2c, W3c, selT, sel, isx, y_out, e_dram, z_dram):
    fp32 = mybir.dt.float32
    i32 = mybir.dt.int32
    ALU = mybir.AluOpType
    ACT = mybir.ActivationFunctionType
    X = mybir.AxisListType.X

    ctx = ExitStack()
    with ctx:
        def sb(name, shape, dt=fp32):
            return ctx.enter_context(nc.sbuf_tensor(name, shape, dt))

        def ps(name, shape):
            return ctx.enter_context(nc.psum_tensor(name, shape, fp32))

        def sem(name):
            return ctx.enter_context(nc.semaphore(name))

        ident = sb("ident", [128, 128])
        ones = sb("ones", [128, 128])
        avg = sb("avg", [128, 128])
        eps = sb("eps", [128, 2])
        blockmask = sb("blockmask", [JN, J])
        ws = sb("ws", [E, D])
        wsc2 = sb("wsc2", [E, 2, D])
        wscg2 = sb("wscg2", [E, 2, D])
        gram = sb("gram", [128, 128])
        lhs0 = sb("lhs0", [128, E])
        lhs1 = sb("lhs1", [128, E])
        wsi4 = sb("wsi4", [JN, P])
        wsisum = sb("wsisum", [JN, 1])
        mixw = sb("mixw", [JN, J, P])
        wd = sb("wd", [128, 2, E])
        wdsum = sb("wdsum", [128, 2])
        wl = sb("wl", [128, 5, OUT_LN])
        wlg = sb("wlg", [128, 5, OUT_LN])
        selT_sb = sb("selT_sb", [P, 2, 5 * 128])
        sel_sb = sb("sel_sb", [128, 2, 5, P])
        isx_sb = sb("isx_sb", [128, 5])
        gb = sb("gb", [P, 2])
        pv = sb("pv", [128, 5, 4])
        pg = sb("pg", [128, 4, 5])
        dext = sb("dext", [128, 5, K4])
        dtmp = sb("dtmp", [128, P])
        vecs = sb("vecs", [128, 4])
        gl_sb = sb("gl_sb", [128, 3])
        bl_sb = sb("bl_sb", [128, 3])
        w1 = sb("w1", [128, 5, H1])
        w2 = sb("w2", [128, 4, H2])
        w3 = sb("w3", [128, 2])
        b1 = sb("b1", [128, 4])
        b2 = sb("b2", [128, 2])
        dt_all = sb("dt_all", [128, 2, B])
        xr = sb("xr", [128, 512])
        xsq = sb("xsq", [128, 512])
        xrs = sb("xrs", [128, 512])
        x_all = sb("x_all", [E, B])
        sx_all = sb("sx_all", [TB, NT])
        idx_all = sb("idx_all", [TB, NT, NS], i32)
        idx = [sb(f"idx{v}", [TB, NS], i32) for v in range(2)]
        e_sb = [sb(f"e_sb{v}", [TB, NS * D]) for v in range(2)]
        eT = sb("eT", [128, NPAIR, TB])
        ege = sb("ege", [TB, NS, D])
        var1 = sb("var1", [TB, NS])
        sd1 = sb("sd1", [TB, NS])
        rstd1 = sb("rstd1", [TB, NS])
        es_sb = [sb(f"es_sb{v}", [TB, NS * D]) for v in range(2)]
        en_sb = [sb(f"en_sb{v}", [JN, G, D]) for v in range(2)]
        m0 = [sb(f"m0_{v}", [128, 512]) for v in range(2)]
        m1 = [sb(f"m1_{v}", [128, 512]) for v in range(2)]
        sq = sb("sq", [E, 2, 512])
        ssq = sb("ssq", [E, 2, 16])
        sd2 = sb("sd2", [E, 2, 16])
        rstd2 = sb("rstd2", [E, 2, 16])
        T = sb("T", [E, G, TW])
        zs = [sb(f"zs{v}", [JP, G, W34]) for v in range(2)]
        zb = [sb(f"zb{v}", [TB, P, W34]) for v in range(2)]
        cz = sb("cz", [TB, 5 * 128])
        xt = sb("xt", [128, 5, TB])
        bn6 = sb("bn6", [TB, 6])
        mv = sb("mv", [TB, 2])
        sd3 = sb("sd3", [TB, 1])
        rstd3 = sb("rstd3", [TB, 1])
        z_sb = sb("z_sb", [TB, DIMS])
        hT = sb("hT", [128, 3, 2, TB])
        h1T = sb("h1T", [128, 4, 2 * TB])
        h2T = sb("h2T", [128, 2, 2 * TB])
        y_sb = sb("y_sb", [1, B])

        pA = ps("pA", [128, 2, 512])
        pM = ps("pM", [128, 512])
        pY = ps("pY", [128, 2, 512])
        pZ = ps("pZ", [128, 4, 256])
        pW = ps("pW", [128, 512])

        w_in = sem("w_in")
        dt_in = sem("dt_in")
        ids_in = sem("ids_in")
        consts_ready = sem("consts_ready")
        prep_dve = sem("prep_dve")
        prep_pe = sem("prep_pe")
        prep_act = sem("prep_act")
        prep_pool = sem("prep_pool")
        consts_chain = sem("consts_chain")
        sp_step = sem("sp_step")
        pool_step = sem("pool_step")
        dve_step = sem("dve_step")
        idx_ready = sem("idx_ready")
        gathered = [sem(f"gathered{v}") for v in range(2)]
        tr_full = sem("tr_full")
        et_ready = sem("et_ready")
        gram_full = sem("gram_full")
        ege_ready = sem("ege_ready")
        var1_ready = sem("var1_ready")
        sd1_ready = sem("sd1_ready")
        scaled = sem("scaled")
        es_stored = [sem(f"es_stored{v}") for v in range(2)]
        en_loaded = [sem(f"en_loaded{v}") for v in range(2)]
        mix_full = sem("mix_full")
        m_ready = sem("m_ready")
        y_full = sem("y_full")
        sq_ready = sem("sq_ready")
        ssq_ready = sem("ssq_ready")
        sd2_ready = sem("sd2_ready")
        rstd2_ready = sem("rstd2_ready")
        t_ready = sem("t_ready")
        xcol_ready = sem("xcol_ready")
        z_full = sem("z_full")
        zs_act = sem("zs_act")
        zs_dve = sem("zs_dve")
        zs_stored = [sem(f"zs_stored{v}") for v in range(2)]
        zb_loaded = [sem(f"zb_loaded{v}") for v in range(2)]
        cz_dve = sem("cz_dve")
        cz_act = sem("cz_act")
        pair_full = sem("pair_full")
        xt_ready = sem("xt_ready")
        out_full = sem("out_full")
        bn_ready = sem("bn_ready")
        ln3_ready = sem("ln3_ready")
        sd3_ready = sem("sd3_ready")
        z_ready = sem("z_ready")
        zt_full = sem("zt_full")
        hT_ready = sem("hT_ready")
        h1_full = sem("h1_full")
        h1_ready = sem("h1_ready")
        h2_full = sem("h2_full")
        h2_ready = sem("h2_ready")
        top_full = sem("top_full")
        y_ready = sem("y_ready")
        y_stored = sem("y_stored")

        block = ctx.enter_context(nc.Block())

        def exists(t):
            return not isinstance(t, int) or 0 <= t < NT

        def later(n):
            return not isinstance(n, int) or n > 0

        def tiles(eng, tile):
            tile(-1, 1)
            tile(0, 0)
            tile(0, 1)
            with eng.Fori(1, NT // 2 - 1) as i:
                tile(i, 0)
                tile(i, 1)
            for i in (NT // 2 - 1, NT // 2):
                tile(i, 0)
                tile(i, 1)

        def rects(v, size):
            base = zb[v][:, 0:1, 0:1]
            free = [[2 * size * (W34 + 1), P // (2 * size)]] + ([[W34, size], [1, size]] if size > 1 else [])
            return bass.AP(tensor=base.tensor, offset=base.offset + size * W34, ap=[base.ap[0]] + free)

        weights_dmas = [
            (ws[:, :], Ws), (vecs[:, 2:3], gs), (lhs0[D:D + 1, :], bs), (lhs1[0:1, :], bs),
            (wsi4[0:NS, :], WsiT), (wsi4[NS:2 * NS, :], WsiT), (wsi4[2 * NS:3 * NS, :], WsiT),
            (wsi4[3 * NS:4 * NS, :], WsiT), (wd[:, :, :], WdT.rearrange("(k p) e -> p k e", p=128)),
            (vecs[:, 0:1], gd), (vecs[:, 1:2], bd),
            (gb[:, 0:1], gsi), (gb[:, 1:2], bsi),
            (selT_sb[:, :, :], selT), (sel_sb[:, :, :, :], sel), (isx_sb[:, :], isx),
            (wl[:, 0:4, :], WlT[0:512, :].rearrange("(k p) m -> p k m", p=128)),
            (wl[N_EXT:K4, 4, :], WlT[512:528, :]),
            (gl_sb[:, :], glc), (bl_sb[:, :], blc),
            (w1[:, 0:3, :], W1[0:DIMS, :].rearrange("(k p) m -> p k m", p=128)),
            (w1[:, 3:5, :], W1[OUT_LN:OUT_LN + KD, :].rearrange("(k p) m -> p k m", p=128)),
            (w2[:, :, :], W2.rearrange("(k p) m -> p k m", p=128)),
            (w3[:, :], W3c), (b1[:, :], b1c), (b2[:, :], b2c),
        ]
        W_ALL = 16 * len(weights_dmas)

        @block.sync
        def _(sp):
            sp.dma_start(idx_all[:, :, :], ids.rearrange("(t p) n -> p t n", p=TB)).then_inc(ids_in, 16)
            sp.dma_start(dt_all[:, :, :], dT.rearrange("(k p) b -> p k b", p=128)).then_inc(dt_in, 16)
            sp.wait_ge(consts_ready, 2)
            for dst, src in weights_dmas:
                sp.dma_start(dst, src).then_inc(w_in, 16)

            def tile(i, u):
                t = 2 * i + u
                v = 1 - u
                if exists(t - 1):
                    sp.wait_ge(zs_act, 32 * t)
                    sp.wait_ge(zs_dve, 32 * t)
                    sp.sem_inc(sp_step, 1)
                    sp.dma_start(z_dram[bass.ds(t - 1, 1)].rearrange("o g j p q -> (o j p) g q"),
                                 zs[v][:, :, :]).then_inc(zs_stored[v], 16)
                    sp.wait_ge(zs_stored[v], 16 * (i + u))
                    sp.sem_inc(sp_step, 1)
                    if later(t - 2):
                        sp.wait_ge(cz_dve, 7 * (t - 2))
                        sp.sem_inc(sp_step, 1)
                        sp.wait_ge(cz_act, 2 * (t - 2))
                    sp.sem_inc(sp_step, 1)
                    sp.dma_start(zb[v][:, :, :],
                                 z_dram[bass.ds(t - 1, 1)].rearrange("o g j p q -> (o g j) p q"))\
                      .then_inc(zb_loaded[v], 16)
                if exists(t + 1):
                    sp.wait_ge(scaled, t + 2)
                    sp.sem_inc(sp_step, 1)
                    sp.dma_start(e_dram[bass.ds(t + 1, 1)].rearrange("o (b n) d -> (o b) (n d)", n=NS),
                                 es_sb[v][:, :]).then_inc(es_stored[v], 16)
                    sp.wait_ge(es_stored[v], 16 * (i + u + 1))
                    sp.sem_inc(sp_step, 1)
                    if later(4 * t):
                        sp.wait_ge(mix_full, 4 * t)
                    sp.sem_inc(sp_step, 1)
                    sp.dma_start(en_sb[v][:, :, :],
                                 e_dram[bass.ds(t + 1, 1)].rearrange("o (g k) d -> (o k) g d", k=JN))\
                      .then_inc(en_loaded[v], 16)

            tiles(sp, tile)
            sp.wait_ge(y_ready, NT // 2)
            sp.dma_start(y_out.rearrange("b o -> o b"), y_sb[:, :]).then_inc(y_stored, 16)
            sp.wait_ge(y_stored, 16)

        @block.gpsimd
        def _(pool):
            nc.gpsimd.memset(ident[:, :], 0.0).then_inc(prep_pool, 1)
            nc.gpsimd.memset(blockmask[:, :], 1.0).then_inc(prep_pool, 1)
            pool.wait_ge(prep_pool, 2)
            nc.gpsimd.affine_select(out=ident[:, :], in_=ident[:, :], compare_op=ALU.not_equal, fill=1.0,
                                    base=0, pattern=[[-1, 128]], channel_multiplier=1).then_inc(prep_pool, 1)
            nc.gpsimd.affine_select(out=blockmask[:, :], in_=blockmask[:, :], compare_op=ALU.is_ge, fill=0.0,
                                    base=0, pattern=[[-NS, J]], channel_multiplier=1).then_inc(prep_pool, 1)
            pool.wait_ge(prep_pool, 4)
            nc.gpsimd.affine_select(out=blockmask[:, :], in_=blockmask[:, :], compare_op=ALU.is_ge, fill=0.0,
                                    base=NS - 1, pattern=[[NS, J]], channel_multiplier=-1).then_inc(prep_pool, 1)
            pool.wait_ge(ids_in, 16)

            def gather(i, v):
                t = 2 * i + v
                if later(16 * NS * i):
                    pool.wait_ge(gathered[v], 16 * NS * i)
                nc.gpsimd.tensor_copy(idx[v][:, :], idx_all[:, bass.ds(t, 1), :].rearrange("p o n -> p (o n)"))\
                  .then_inc(idx_ready, 1)
                pool.wait_ge(idx_ready, t + 1)
                if later(t - 1):
                    pool.wait_ge(scaled, t - 1)
                pool.sem_inc(pool_step, 1)
                for n in range(NS):
                    pool.indirect_dma_start(
                        out=e_sb[v][:, n * D:(n + 1) * D], out_offset=None, in_=tables[n],
                        in_offset=bass.IndirectOffsetOnAxis(ap=idx[v][:, n:n + 1], axis=0))\
                        .then_inc(gathered[v], 16)

            gather(0, 0)
            gather(0, 1)
            with pool.Fori(1, NT // 2) as i:
                gather(i, 0)
                gather(i, 1)

        @block.tensor
        def _(pe):
            mm = nc.tensor.matmul
            pe.wait_ge(w_in, W_ALL)
            pe.wait_ge(consts_ready, 2)
            pe.wait_ge(prep_pool, 5)
            mm(pW[:, 0:D], avg[:, :], ws[:, :], start=True, stop=True).then_inc(prep_pe, 1)
            pe.wait_ge(prep_dve, 1)
            for k in range(5):
                for h in range(2):
                    last = mm(pM[:, 4 * k + 2 * h:4 * k + 2 * h + 2], selT_sb[:, h, 128 * k:128 * (k + 1)],
                              gb[:, :], start=True, stop=True)
            last.then_inc(prep_pe, 1)
            pe.wait_ge(prep_dve, 2)
            wsc_flat = wsc2[:, :, :].rearrange("e a d -> e (a d)")
            mm(pA[:, 0, 0:128], wsc_flat, wsc_flat, start=True, stop=True).then_inc(prep_pe, 1)
            nc.tensor.transpose(pA[:, 1, 0:128], wscg2[:, :, :].rearrange("e a d -> e (a d)"), ident[:, :])\
              .then_inc(prep_pe, 1)
            pe.wait_ge(prep_dve, 3)
            mm(pW[:, 128:256], ones[0:JN, :], mixw[:, :, :].rearrange("k j p -> k (j p)"), start=True, stop=True)\
                .then_inc(prep_pe, 1)
            pe.wait_ge(prep_dve, 4)
            for k in range(5):
                rows = 128 if k < 4 else K4
                last = mm(pZ[0:K4, 0:2, :], dext[0:rows, k, :], wl[0:rows, k, :], start=(k == 0), stop=(k == 4))
            last.then_inc(prep_pe, 1)
            pe.wait_ge(dt_in, 16)
            for c in range(B // 512):
                if c:
                    pe.wait_ge(prep_act, 4 * c)
                for k in range(2):
                    last = mm(pY[:, 0, :], wd[:, k, :], dt_all[:, k, 512 * c:512 * (c + 1)],
                              start=(k == 0), stop=(k == 1))
                last.then_inc(prep_pe, 1)
                pe.wait_ge(prep_act, 4 * c + 2)
                mm(pY[:, 1, :], avg[:, :], xsq[:, :], start=True, stop=True).then_inc(prep_pe, 1)
            pe.wait_ge(prep_act, 4 * (B // 512))
            for t in range(NT):
                last = mm(pM[:, t:t + 1], x_all[:, TB * t:TB * (t + 1)], ones[:, 0:1], start=True, stop=True)
            last.then_inc(prep_pe, 1)
            pe.wait_ge(prep_dve, 5 + 2 * (B // 512) + 1)

            def tile(i, u):
                t = 2 * i + u
                s = t + 1
                v = 1 - u

                def z_fill(c, f):
                    tz, c1 = (t, c - 1) if c else (t - 1, CH - 1)
                    if not exists(tz):
                        return
                    if f == 0:
                        pe.wait_ge(t_ready, 8 * tz + 2 * c1 + 2)
                        pe.wait_ge(xcol_ready, 4 * tz + c1 + 1)
                    if later(32 * tz + 8 * c1 + 4 * f):
                        pe.wait_ge(zs_act, 32 * tz + 8 * c1 + 4 * f)
                        pe.wait_ge(zs_dve, 32 * tz + 8 * c1 + 4 * f)
                    for a in range(4):
                        g = GC * c1 + 4 * f + a
                        last = mm(pZ[:, a, 0:TW], T[:, g, 0:JP], T[:, g, :], start=True, stop=True)
                    last.then_inc(z_full, 1)

                def ln1_transpose(q):
                    if not exists(s):
                        return
                    if q == 0:
                        pe.wait_ge(gathered[v], 16 * NS * (i + u + 1))
                    if q < 2:
                        if later(4 * s):
                            pe.wait_ge(ege_ready, 4 * s)
                    else:
                        pe.wait_ge(et_ready, 4 * s + q - 1)
                    for a in range(4 * q, min(4 * q + 4, NPAIR)):
                        last = nc.tensor.transpose(pA[:, q % 2, 128 * (a - 4 * q):128 * (a - 4 * q + 1)],
                                                   e_sb[v][:, 128 * a:128 * (a + 1)], ident[:, :])
                    last.then_inc(tr_full, 1)

                def ln1_gram(q):
                    if not exists(s):
                        return
                    if q < 2:
                        pe.wait_ge(et_ready, 4 * s + q + 3)
                    else:
                        pe.wait_ge(ege_ready, 4 * s + q - 1)
                    for a in range(4 * q, min(4 * q + 4, NPAIR)):
                        last = mm(pA[:, q % 2, 128 * (a - 4 * q):128 * (a - 4 * q + 1)], eT[:, a, :], gram[:, :],
                                  start=True, stop=True)
                    last.then_inc(gram_full, 1)

                def pairs_first():
                    if not exists(t - 1):
                        return
                    pe.wait_ge(cz_dve, 7 * t)
                    pe.wait_ge(cz_act, 2 * t)
                    if u == 1 and exists(t - 3):
                        pe.wait_ge(h2_ready, 2 * i)
                    elif later(3 * (t - 1)):
                        pe.wait_ge(hT_ready, 3 * (t - 1))
                    for k in range(4):
                        last = nc.tensor.transpose(pW[:, 128 * k:128 * (k + 1)], cz[:, 128 * k:128 * (k + 1)],
                                                   ident[:, :])
                    last.then_inc(pair_full, 1)

                def pairs_second():
                    if not exists(t - 1):
                        return
                    pe.wait_ge(xt_ready, 2 * t - 1)
                    nc.tensor.transpose(pW[:, 0:128], cz[:, 512:640], ident[:, :]).then_inc(pair_full, 1)

                def wl_product():
                    if not exists(t - 1):
                        return
                    pe.wait_ge(xt_ready, 2 * t)
                    if u == 1 and exists(t - 3):
                        pe.wait_ge(y_ready, i)
                    for k in range(5):
                        rows = 128 if k < 4 else K4
                        last = mm(pW[:, :], xt[0:rows, k, :], wlg[0:rows, k, :], start=(k == 0), stop=(k == 4))
                    last.then_inc(out_full, 1)

                def z_transpose():
                    if not exists(t - 2):
                        return
                    pe.wait_ge(z_ready, t - 1)
                    for k in range(3):
                        last = nc.tensor.transpose(pW[:, 128 * k:128 * (k + 1)], z_sb[:, 128 * k:128 * (k + 1)],
                                                   ident[:, :])
                    last.then_inc(zt_full, 1)

                def mlp_first(half):
                    if not (u == 1 and exists(t - 3)):
                        return
                    if half == 0:
                        pe.wait_ge(hT_ready, 3 * (t - 1))
                    else:
                        pe.wait_ge(h1_ready, 4 * (i - 1) + 2)
                    for a in range(2):
                        m = 2 * half + a
                        for k in range(5):
                            rhs = hT[:, k, :, :] if k < 3 else dt_all[:, k - 3, bass.ds(TB * (t - 3), 2 * TB)]
                            last = mm(pW[:, 256 * a:256 * (a + 1)], w1[:, k, 128 * m:128 * (m + 1)], rhs,
                                      start=(k == 0), stop=(k == 4))
                    last.then_inc(h1_full, 1)

                def mlp_second():
                    if not (u == 1 and exists(t - 3)):
                        return
                    pe.wait_ge(h1_ready, 4 * i)
                    for m in range(2):
                        for k in range(4):
                            last = mm(pW[:, 256 * m:256 * (m + 1)], w2[:, k, 128 * m:128 * (m + 1)], h1T[:, k, :],
                                      start=(k == 0), stop=(k == 3))
                    last.then_inc(h2_full, 1)

                def mlp_third():
                    if not (u == 1 and exists(t - 3)):
                        return
                    pe.wait_ge(h2_ready, 2 * i)
                    if exists(t - 1):
                        pe.wait_ge(xt_ready, 2 * t)
                    for k in range(2):
                        last = mm(pW[0:1, 0:256], w3[:, k:k + 1], h2T[:, k, :], start=(k == 0), stop=(k == 1))
                    last.then_inc(top_full, 1)

                for c in range(CH):
                    n = 4 * t + c
                    if c == 0:
                        z_transpose()
                    if c == 2:
                        mlp_second()
                    if c == 3:
                        mlp_third()
                    if exists(t):
                        if c == 0:
                            pe.wait_ge(en_loaded[u], 16 * (i + 1))
                        if later(2 * n):
                            pe.wait_ge(m_ready, 2 * n)
                        for k in range(4):
                            g = GC * c + 2 * k
                            last = mm(pM[:, 128 * k:128 * (k + 1)], en_sb[u][:, g:g + 2, :],
                                      mixw[:, :, :], start=True, stop=True)
                        last.then_inc(mix_full, 1)
                    z_fill(c, 0)
                    if exists(t):
                        pe.wait_ge(m_ready, 2 * n + 2)
                        for h in range(2):
                            if later(2 * n + h - 1):
                                pe.wait_ge(t_ready, 2 * n + h - 1)
                            if h == 0:
                                mm(pY[:, 0, :], lhs0[0:D + 1, :], m0[c % 2][0:D + 1, :], start=True, stop=True)\
                                    .then_inc(y_full, 1)
                            else:
                                mm(pY[:, 1, :], lhs1[:, :], m1[c % 2][:, :], start=True, stop=True)\
                                    .then_inc(y_full, 1)
                    if c == 0:
                        ln1_transpose(0)
                        ln1_transpose(1)
                    if c == 1:
                        ln1_gram(0)
                        ln1_gram(1)
                    if c == 2:
                        pairs_first()
                    if c == 3:
                        wl_product()
                    z_fill(c, 1)
                    if c == 0:
                        ln1_transpose(2)
                        ln1_transpose(3)
                        mlp_first(0)
                    if c == 1:
                        ln1_gram(2)
                        ln1_gram(3)
                        mlp_first(1)
                    if c == 2:
                        pairs_second()

            tiles(pe, tile)

        @block.scalar
        def _(act):
            def copy(out, in_, **k):
                return nc.scalar.activation(out, in_, ACT.Copy, **k)

            for c in range(B // 512):
                act.wait_ge(prep_pe, 7 + 2 * c)
                copy(xr[:, :], pY[:, 0, :]).then_inc(prep_act, 1)
                nc.scalar.activation(xsq[:, :], pY[:, 0, :], ACT.Square).then_inc(prep_act, 1)
                act.wait_ge(prep_pe, 8 + 2 * c)
                nc.scalar.activation(xrs[:, :], pY[:, 1, :], ACT.Sqrt, bias=eps[:, 0:1]).then_inc(prep_act, 1)
                act.wait_ge(prep_dve, 7 + 2 * c)
                nc.scalar.activation(x_all[:, 512 * c:512 * (c + 1)], xr[:, :], ACT.Identity,
                                     bias=vecs[:, 1:2], scale=vecs[:, 0:1]).then_inc(prep_act, 1)

            def tile(i, u):
                t = 2 * i + u
                s = t + 1
                v = 1 - u

                def z_copy(c, f):
                    tz, c1, w = (t, c - 1, u) if c else (t - 1, CH - 1, v)
                    if not exists(tz):
                        return
                    if c1 == 0 and f == 0 and later(16 * i):
                        act.wait_ge(zs_stored[w], 16 * i)
                    act.wait_ge(z_full, 8 * tz + 2 * c1 + f + 1)
                    g = GC * c1 + 4 * f
                    for j in range(2):
                        quad = slice(P * j, P * (j + 1))
                        copy(zs[w][quad, g:g + 4, 0:P], pZ[quad, :, quad]).then_inc(zs_act, 1)
                        copy(zs[w][quad, g:g + 4, P:W34], pZ[quad, :, JP + j:TW:J]).then_inc(zs_act, 1)

                def ln1_copy(q):
                    if not exists(s):
                        return
                    act.wait_ge(tr_full, 4 * s + q + 1)
                    if q == 0 and later(4 * s):
                        act.wait_ge(gram_full, 4 * s)
                    a, n = 4 * q, min(4, NPAIR - 4 * q)
                    copy(eT[:, a:a + n, :], pA[:, q % 2, 0:128 * n]).then_inc(et_ready, 1)

                for c in range(CH):
                    n = 4 * t + c
                    if c == 0 and exists(t - 2):
                        act.wait_ge(zt_full, t - 1)
                        if later(2 * (i - 1)):
                            act.wait_ge(h1_full, 2 * (i - 1))
                        for k in range(3):
                            nc.scalar.activation(hT[:, k, u, :], pW[:, 128 * k:128 * (k + 1)], ACT.Identity,
                                                 bias=bl_sb[:, k:k + 1], scale=gl_sb[:, k:k + 1]).then_inc(hT_ready, 1)
                    if c == 2 and exists(t - 1):
                        act.wait_ge(zb_loaded[v], 16 * (i + u))
                        if later(2 * (t - 1)):
                            act.wait_ge(pair_full, 2 * (t - 1))
                        copy(cz[:, 0:256].rearrange("b (r c) -> b r c", c=16), zb[v][:, 16:32, 0:16]).then_inc(cz_act, 1)
                        copy(cz[:, 256:384].rearrange("b (s r c) -> b s r c", r=8, c=8), rects(v, 8)).then_inc(cz_act, 1)
                    if c == 2 and u == 1 and exists(t - 3):
                        act.wait_ge(h2_full, i)
                        if later(i - 1):
                            act.wait_ge(top_full, i - 1)
                        for m in range(2):
                            nc.scalar.activation(h2T[:, m, :], pW[:, 256 * m:256 * (m + 1)], ACT.Relu,
                                                 bias=b2[:, m:m + 1]).then_inc(h2_ready, 1)
                    if c == 3 and u == 1 and exists(t - 3):
                        act.wait_ge(top_full, i)
                        copy(y_sb[:, bass.ds(TB * (t - 3), 2 * TB)], pW[0:1, 0:256]).then_inc(y_ready, 1)
                    if exists(t):
                        act.wait_ge(mix_full, n + 1)
                        if later(2 * (n - 1)):
                            act.wait_ge(y_full, 2 * (n - 1))
                        copy(m0[c % 2][0:D, :], pM[0:D, :]).then_inc(m_ready, 1)
                        copy(m1[c % 2][D:128, :], pM[D:128, :]).then_inc(m_ready, 1)
                        if later(8 * t + 2 * c - 6):
                            act.wait_ge(z_full, 8 * t + 2 * c - 6)
                        copy(T[:, GC * c:GC * (c + 1), JP:JP + J],
                             x_all[:, bass.ds(TB * t + 32 * c, 32)].rearrange("e (g j) -> e g j", j=J))\
                            .then_inc(xcol_ready, 1)
                    z_copy(c, 0)
                    if exists(t):
                        for h in range(2):
                            act.wait_ge(y_full, 2 * n + h + 1)
                            if later(2 * n + h - 1):
                                act.wait_ge(ssq_ready, 2 * n + h - 1)
                            nc.scalar.activation(sq[:, h, :], pY[:, h, :], ACT.Square).then_inc(sq_ready, 1)
                    if c == 0:
                        ln1_copy(0)
                        ln1_copy(1)
                    if exists(t):
                        act.wait_ge(ssq_ready, 2 * n + 2)
                        if later(n):
                            act.wait_ge(rstd2_ready, n)
                        nc.scalar.activation(sd2[:, :, :], ssq[:, :, :], ACT.Sqrt, bias=eps[:, 1:2]).then_inc(sd2_ready, 1)
                    if c == 3 and exists(t - 1):
                        act.wait_ge(ln3_ready, 2 * t - 1)
                        nc.scalar.activation(sd3[:, :], mv[:, 1:2], ACT.Sqrt, bias=eps[:, 0:1]).then_inc(sd3_ready, 1)
                    if c == 2 and exists(t - 1):
                        act.wait_ge(pair_full, 2 * t - 1)
                        if later(t - 1):
                            act.wait_ge(out_full, t - 1)
                        copy(xt[:, 0:4, :], pW[:, :]).then_inc(xt_ready, 1)
                    z_copy(c, 1)
                    if c == 0:
                        ln1_copy(2)
                        ln1_copy(3)
                    if c == 2 and exists(t - 1):
                        act.wait_ge(pair_full, 2 * t)
                        copy(xt[0:K4, 4, :], pW[0:K4, 0:128]).then_inc(xt_ready, 1)
                    if c < 2 and u == 1 and exists(t - 3):
                        act.wait_ge(h1_full, 2 * (i - 1) + c + 1)
                        if c == 0 and later(i - 1):
                            act.wait_ge(h2_full, i - 1)
                        for a in range(2):
                            m = 2 * c + a
                            nc.scalar.activation(h1T[:, m, :], pW[:, 256 * a:256 * (a + 1)], ACT.Relu,
                                                 bias=b1[:, m:m + 1]).then_inc(h1_ready, 1)
                    if c == 1 and exists(s):
                        act.wait_ge(var1_ready, 3 * s + 2)
                        nc.scalar.activation(sd1[:, :], var1[:, :], ACT.Sqrt, bias=eps[:, 0:1]).then_inc(sd1_ready, 1)

            tiles(act, tile)

        @block.vector
        def _(dve):
            V = nc.vector
            chain = [0]

            def link(ins):
                chain[0] += 1
                ins.then_inc(consts_chain, 1)
                dve.wait_ge(consts_chain, chain[0])

            link(V.memset(lhs1[0:D, :], 0.0))
            V.memset(wl[0:64, 4, :], 0.0).then_inc(consts_ready, 1)
            V.memset(ones[:, :], 1.0)
            V.memset(T[:, :, JP + J:TW], 1.0)
            link(V.memset(cz[:, 512:640], 0.0))
            V.memset(cz[:, 512 + P + 1:512 + P + 2], 1.0)
            V.memset(m1[0][0:D, :], 0.0)
            V.memset(m1[1][0:D, :], 0.0)
            V.memset(gram[:, :], 0.0)
            V.memset(eps[:, 0:1], EPS)
            V.memset(eps[:, 1:2], P * EPS)
            link(V.memset(dext[:, :, :], 0.0))
            V.memset(avg[:, :], 1.0 / E).then_inc(consts_ready, 1)
            dve.wait_ge(w_in, W_ALL)
            dve.wait_ge(prep_pool, 5)
            V.tensor_scalar(gb[:, 0:1], gb[:, 0:1], float(P) ** 0.5, None, ALU.mult).then_inc(prep_dve, 1)
            dve.wait_ge(prep_pe, 1)
            for h in range(2):
                link(V.tensor_tensor(wsc2[:, h, :], ws[:, :], pW[:, 0:D], ALU.subtract))
            V.tensor_scalar(wscg2[:, :, :], wsc2[:, :, :], vecs[:, 2:3], None, ALU.mult).then_inc(prep_dve, 1)
            link(V.tensor_reduce(wsisum[:, :], wsi4[:, :], X, ALU.add))
            link(V.tensor_scalar(wsisum[:, :], wsisum[:, :], -1.0 / P, None, ALU.mult))
            link(V.tensor_scalar(wsi4[:, :], wsi4[:, :], wsisum[:, 0:1], None, ALU.add))
            for j in range(J - 1):
                link(V.tensor_scalar(mixw[:, j, :], wsi4[:, :], blockmask[:, j:j + 1], None, ALU.mult))
            V.tensor_scalar(mixw[:, J - 1, :], wsi4[:, :], blockmask[:, J - 1:J], None, ALU.mult)\
                .then_inc(prep_dve, 1)
            link(V.tensor_reduce(wdsum[:, :], wd[:, :, :], X, ALU.add))
            link(V.tensor_scalar(wdsum[:, :], wdsum[:, :], -1.0 / E, None, ALU.mult))
            for k in range(2):
                link(V.tensor_scalar(wd[:, k, :], wd[:, k, :], wdsum[:, k:k + 1], None, ALU.add))
            dve.wait_ge(prep_pe, 2)
            link(V.tensor_copy(pv[:, :, :], pM[:, 0:20].rearrange("p (k a) -> p k a", a=4)))
            gp, bp, gq, bq = (pv[:, :, a] for a in range(4))
            link(V.tensor_tensor(pg[:, 3, :], gq, isx_sb[:, :], ALU.add))
            link(V.tensor_tensor(pg[:, 0, :], gp, pg[:, 3, :], ALU.mult))
            link(V.tensor_tensor(pg[:, 1, :], gp, bq, ALU.mult))
            link(V.tensor_tensor(pg[:, 2, :], gq, bp, ALU.mult))
            link(V.tensor_tensor(dext[:, :, P], isx_sb[:, :], bp, ALU.mult))
            link(V.scalar_tensor_tensor(dext[:, :, P + 1], bp, float(E), bq, ALU.mult, ALU.mult))
            for k in range(5):
                link(V.tensor_scalar(dtmp[:, :], sel_sb[:, 0, k, :], pg[:, 1, k:k + 1], None, ALU.mult))
                ins = V.scalar_tensor_tensor(dext[:, k, 0:P], sel_sb[:, 1, k, :], pg[:, 2, k:k + 1], dtmp[:, :],
                                             ALU.mult, ALU.add)
                if k < 4:
                    link(ins)
                else:
                    ins.then_inc(prep_dve, 1)
            dve.wait_ge(prep_pe, 4)
            for h in range(2):
                q = slice(D * h, D * (h + 1))
                link(V.tensor_scalar(gram[q, q], pA[q, 0, q], 1.0 / E, None, ALU.mult))
            link(V.tensor_copy(lhs0[0:D, :], pA[0:D, 1, 0:128]))
            link(V.tensor_copy(lhs1[D:128, :], pA[D:128, 1, 0:128]))
            dve.wait_ge(prep_pe, 5)
            for r in range(4):
                for w in range(2):
                    link(V.tensor_copy(m0[w][D:D + 1, 128 * r:128 * (r + 1)], pW[D:D + 1, 128:256]))
                    link(V.tensor_copy(m1[w][0:1, 128 * r:128 * (r + 1)], pW[0:1, 128:256]))
            dve.wait_ge(prep_pe, 6)
            for k in range(4):
                link(V.tensor_scalar(wlg[:, k, :], wl[:, k, :], pg[:, 0, k:k + 1], None, ALU.mult))
            V.scalar_tensor_tensor(wlg[0:K4, 4, :], wl[0:K4, 4, :], pg[0:K4, 0, 4:5],
                                   pZ[0:K4, 0:2, :].rearrange("p a m -> p (a m)"), ALU.mult, ALU.add)\
                .then_inc(prep_dve, 1)
            for c in range(B // 512):
                dve.wait_ge(prep_act, 4 * c + 3)
                V.reciprocal(xrs[:, :], xrs[:, :]).then_inc(prep_dve, 1)
                dve.wait_ge(prep_dve, 6 + 2 * c)
                V.tensor_tensor(xr[:, :], xr[:, :], xrs[:, :], ALU.mult).then_inc(prep_dve, 1)
            dve.wait_ge(prep_pe, 7 + 2 * (B // 512))
            V.tensor_copy(sx_all[:, :], pM[:, 0:NT]).then_inc(prep_dve, 1)

            def tile(i, u):
                t = 2 * i + u
                s = t + 1
                v = 1 - u

                def z_copy(c, f):
                    tz, c1, w = (t, c - 1, u) if c else (t - 1, CH - 1, v)
                    if not exists(tz):
                        return
                    if c1 == 0 and f == 0 and later(16 * i):
                        dve.wait_ge(zs_stored[w], 16 * i)
                    dve.wait_ge(z_full, 8 * tz + 2 * c1 + f + 1)
                    g = GC * c1 + 4 * f
                    for j in range(2, 4):
                        quad = slice(P * j, P * (j + 1))
                        V.tensor_copy(zs[w][quad, g:g + 4, 0:P], pZ[quad, :, quad]).then_inc(zs_dve, 1)
                        V.tensor_copy(zs[w][quad, g:g + 4, P:W34], pZ[quad, :, JP + j:TW:J]).then_inc(zs_dve, 1)

                def ln1_product(q):
                    if not exists(s):
                        return
                    if q == 0:
                        dve.wait_ge(gathered[v], 16 * NS * (i + u + 1))
                    dve.wait_ge(gram_full, 4 * s + q + 1)
                    a, n = 512 * q, min(512, NS * D - 512 * q)
                    flat = ege[:, :, :].rearrange("b n d -> b (n d)")
                    V.tensor_tensor(flat[:, a:a + n], pA[:, q % 2, 0:n], e_sb[v][:, a:a + n], ALU.mult)\
                        .then_inc(ege_ready, 1)

                def ln1_finish():
                    if not exists(s):
                        return
                    dve.wait_ge(ege_ready, 4 * s + 4)
                    V.tensor_reduce(var1[:, :], ege[:, :, :], X, ALU.add).then_inc(var1_ready, 1)
                    dve.wait_ge(var1_ready, 3 * s + 1)
                    V.tensor_scalar(var1[:, :], var1[:, :], 0.0, None, ALU.max).then_inc(var1_ready, 1)
                    compact()
                    dve.wait_ge(sd1_ready, s + 1)
                    V.reciprocal(rstd1[:, :], sd1[:, :]).then_inc(var1_ready, 1)
                    dve.wait_ge(var1_ready, 3 * s + 3)
                    if later(16 * (i + u)):
                        dve.wait_ge(es_stored[v], 16 * (i + u))
                    V.tensor_tensor(es_sb[v][:, :].rearrange("b (n d) -> b n d", d=D),
                                    e_sb[v][:, :].rearrange("b (n d) -> b n d", d=D),
                                    rstd1[:, :].unsqueeze(2).to_broadcast([TB, NS, D]), ALU.mult).then_inc(scaled, 1)

                def compact():
                    if not exists(t - 1):
                        return
                    dve.wait_ge(zb_loaded[v], 16 * (i + u))
                    if later(2 * (t - 1)):
                        dve.wait_ge(pair_full, 2 * (t - 1))
                    V.tensor_copy(cz[:, 384:448].rearrange("b (s r c) -> b s r c", r=4, c=4), rects(v, 4)).then_inc(cz_dve, 1)
                    V.tensor_copy(cz[:, 448:480].rearrange("b (s r c) -> b s r c", r=2, c=2), rects(v, 2)).then_inc(cz_dve, 1)
                    V.tensor_copy(cz[:, 480:496], rects(v, 1)).then_inc(cz_dve, 1)
                    V.tensor_copy(cz[:, 496:512], zb[v][:, 0:16, P]).then_inc(cz_dve, 1)
                    V.tensor_copy(cz[:, 512 + N_EXT:512 + K4], zb[v][:, 16:32, P]).then_inc(cz_dve, 1)
                    V.tensor_copy(cz[:, 512:512 + P], zb[v][:, :, P + 1]).then_inc(cz_dve, 1)
                    V.tensor_copy(cz[:, 512 + P:512 + P + 1], sx_all[:, bass.ds(t - 1, 1)]).then_inc(cz_dve, 1)

                def ln3():
                    if not exists(t - 1):
                        return
                    dve.wait_ge(out_full, t)
                    V.bn_stats(bn6[:, :], pW[:, :]).then_inc(bn_ready, 1)
                    dve.wait_ge(bn_ready, t)
                    dve.sem_inc(dve_step, 1)
                    V.bn_aggr(mv[:, :], bn6[:, :]).then_inc(ln3_ready, 1)
                    dve.wait_ge(sd3_ready, t)
                    V.reciprocal(rstd3[:, :], sd3[:, :]).then_inc(ln3_ready, 1)
                    dve.wait_ge(ln3_ready, 2 * t)
                    if later(t - 1):
                        dve.wait_ge(zt_full, t - 1)
                    V.tensor_scalar(z_sb[:, :], pW[:, 0:DIMS], mv[:, 0:1], rstd3[:, 0:1], ALU.subtract, ALU.mult)\
                        .then_inc(z_ready, 1)

                for c in range(CH):
                    n = 4 * t + c
                    z_copy(c, 0)
                    if exists(t):
                        for h in range(2):
                            dve.wait_ge(sq_ready, 2 * n + h + 1)
                            V.tensor_reduce(ssq[:, h, :], sq[:, h, :].rearrange("e (b p) -> e b p", p=P), X, ALU.add)\
                                .then_inc(ssq_ready, 1)
                    if c == 1:
                        ln1_product(0)
                        ln1_product(1)
                    if exists(t):
                        dve.wait_ge(sd2_ready, n + 1)
                        V.reciprocal(rstd2[:, :, :], sd2[:, :, :]).then_inc(rstd2_ready, 1)
                        dve.wait_ge(rstd2_ready, n + 1)
                        if later(8 * t + 2 * c - 6):
                            dve.wait_ge(z_full, 8 * t + 2 * c - 6)
                        for h in range(2):
                            V.tensor_tensor(T[:, GC * c + h:GC * (c + 1):2, 0:JP].rearrange("e k (j p) -> e k j p", p=P),
                                            pY[:, h, :].rearrange("e (k j p) -> e k j p", j=J, p=P),
                                            rstd2[:, h, :].rearrange("e (k j) -> e k j", j=J).unsqueeze(3)
                                            .to_broadcast([E, 4, J, P]), ALU.mult).then_inc(t_ready, 1)
                    if c == 3:
                        ln3()
                    z_copy(c, 1)
                    if c == 1:
                        ln1_product(2)
                        ln1_product(3)
                        ln1_finish()
                        if not exists(s):
                            compact()

            tiles(dve, tile)


def kernel(**inputs):
    import concourse.bacc as bacc
    from concourse.bass_utils import run_bass_kernel_spmd as run

    nc = bacc.Bacc("TRN2", target_bir_lowering=False, num_devices=1)
    blocks = pair_blocks()
    f32 = np.float32
    selT = np.zeros((P, 2, 5 * 128), f32)
    sel = np.zeros((128, 2, 5, P), f32)
    isx = np.zeros((128, 5), f32)
    columns = []
    for k, rows in enumerate(blocks):
        for r, pair in enumerate(rows):
            if pair is None:
                continue
            p, q = pair
            columns.append(p * (p + 1) // 2 + q + 1)
            for h, c in ((0, p), (1, q)):
                if c >= 0:
                    selT[c, h, 128 * k + r] = 1
                    sel[r, h, k, c] = 1
            isx[r, k] = q < 0
    a = {k: np.asarray(v) for k, v in inputs.items()}
    col = lambda x: x.reshape(-1, 1)
    blocked = lambda x: np.ascontiguousarray(x.reshape(-1, 128).T)
    arrays = {
        "ids": a["ids"],
        **{f"tbl_{n}": a[f"tbl_{n}"] for n in range(NS)},
        "dT": a["r_dense_t"].T, "WdT": a["L0_rec_Wd"].T, "gd": col(a["L0_rec_gd"]), "bd": col(a["L0_rec_bd"]),
        "Ws": a["L0_rec_Ws"], "gs": col(a["L0_rec_gs"]), "bs": a["L0_rec_bs"].reshape(1, -1),
        "WsiT": a["L0_rec_Wsi"].T, "gsi": col(a["L0_rec_gsi"]), "bsi": col(a["L0_rec_bsi"]),
        "WlT": a["L0_rec_Wl"].T[columns], "glc": blocked(a["L0_rec_gl"][:DIMS]),
        "blc": blocked(a["L0_rec_bl"][:DIMS]),
        "W1": a["W_top1"], "b1c": blocked(a["b_top1"]), "W2": a["W_top2"], "b2c": blocked(a["b_top2"]),
        "W3c": blocked(a["W_top3"]), "selT": selT, "sel": sel, "isx": isx,
    }
    arrays = {k: np.ascontiguousarray(v) for k, v in arrays.items()}
    aps = {k: nc.dram_tensor(k, v.shape, mybir.dt.from_np(v.dtype), kind="ExternalInput").ap()
           for k, v in arrays.items()}
    tables = [aps.pop(f"tbl_{n}") for n in range(NS)]
    y = nc.dram_tensor("y", (B, 1), mybir.dt.float32, kind="ExternalOutput").ap()
    e_dram = nc.dram_tensor("e_dram", (NT, TB * NS, D), mybir.dt.float32, kind="Internal").ap()
    z_dram = nc.dram_tensor("z_dram", (NT, G, J, P, W34), mybir.dt.float32, kind="Internal").ap()
    build(nc, tables=tables, y_out=y, e_dram=e_dram, z_dram=z_dram, **aps)
    r = run(nc, [arrays], core_ids=[0])
    return r.results[0]["y"]
```

```python
import numpy as np
import concourse.bass as bass
from concourse import mybir
from contextlib import ExitStack

VOCABS = [12500, 1250, 125000, 1250, 1000, 12500, 1000, 12500, 125000, 1000, 1250, 1000, 1250,
          1000, 1000, 12500, 125000, 12500, 12500, 1000, 1000, 12500, 1000, 1000, 1000, 12500]
B, NS, D, E, P, KD = 2048, 26, 64, 128, 32, 256
OUT_LN, DIMS, H1, H2 = 512, 384, 512, 256
TB = 128
NT = B // TB
J = 4
G = TB // J
CH = 4
GC = G // CH
JN = J * NS
JP = J * P
W34 = P + 2
TW = J * W34
NPAIR = NS // 2
EPS = 1e-5
N_EXT = P + 2
K4 = N_EXT + P // 2


def pair_blocks():
    blocks = [[(p, q) for p in range(16, 24) for q in range(16)],
              [(p, q) for p in range(24, 32) for q in range(16)],
              [(16 * s + 8 + r, 16 * s + c) for s in range(2) for r in range(8) for c in range(8)],
              [(8 * s + 4 + r, 8 * s + c) for s in range(4) for r in range(4) for c in range(4)]
              + [(4 * s + 2 + r, 4 * s + c) for s in range(8) for r in range(2) for c in range(2)]
              + [(2 * s + 1, 2 * s) for s in range(16)] + [(p, -1) for p in range(16)],
              [None] * N_EXT + [(p, -1) for p in range(16, 32)]]
    return blocks


def build(nc, ids, tables, dT, WdT, gd, bd, Ws, gs, bs, WsiT, gsi, bsi, WlT, glc, blc,
          W1, b1c, W2, b2c, W3c, selT, sel, isx, y_out, e_dram, z_dram):
    fp32 = mybir.dt.float32
    i32 = mybir.dt.int32
    ALU = mybir.AluOpType
    ACT = mybir.ActivationFunctionType
    X = mybir.AxisListType.X

    ctx = ExitStack()
    with ctx:
        def sb(name, shape, dt=fp32):
            return ctx.enter_context(nc.sbuf_tensor(name, shape, dt))

        def ps(name, shape):
            return ctx.enter_context(nc.psum_tensor(name, shape, fp32))

        def sem(name):
            return ctx.enter_context(nc.semaphore(name))

        ident = sb("ident", [128, 128])
        ones = sb("ones", [128, 128])
        avg = sb("avg", [128, 128])
        eps = sb("eps", [128, 2])
        blockmask = sb("blockmask", [JN, J])
        ws = sb("ws", [E, D])
        wsc2 = sb("wsc2", [E, 2, D])
        wscg2 = sb("wscg2", [E, 2, D])
        gram = sb("gram", [128, 128])
        lhs0 = sb("lhs0", [128, E])
        lhs1 = sb("lhs1", [128, E])
        wsi4 = sb("wsi4", [JN, P])
        wsisum = sb("wsisum", [JN, 1])
        mixw = sb("mixw", [JN, J, P])
        wd = sb("wd", [128, 2, E])
        wdsum = sb("wdsum", [128, 2])
        wl = sb("wl", [128, 5, OUT_LN])
        wlg = sb("wlg", [128, 5, OUT_LN])
        selT_sb = sb("selT_sb", [P, 2, 5 * 128])
        sel_sb = sb("sel_sb", [128, 2, 5, P])
        isx_sb = sb("isx_sb", [128, 5])
        gb = sb("gb", [P, 2])
        pv = sb("pv", [128, 5, 4])
        pg = sb("pg", [128, 4, 5])
        dext = sb("dext", [128, 5, K4])
        dtmp = sb("dtmp", [128, 5, P])
        vecs = sb("vecs", [128, 4])
        gl_sb = sb("gl_sb", [128, 3])
        bl_sb = sb("bl_sb", [128, 3])
        w1 = sb("w1", [128, 5, H1])
        w2 = sb("w2", [128, 4, H2])
        w3 = sb("w3", [128, 2])
        b1 = sb("b1", [128, 4])
        b2 = sb("b2", [128, 2])
        dt_all = sb("dt_all", [128, 2, B])
        xsq = sb("xsq", [TB, 2, 4, E])
        xss = sb("xss", [TB, NT])
        xsd = sb("xsd", [TB, NT])
        xrstd = sb("xrstd", [TB, NT])
        xr = sb("xr", [TB, 2, 4, E])
        x_all = sb("x_all", [E, B])
        sx_all = sb("sx_all", [TB, NT])
        idx_all = sb("idx_all", [TB, NT, NS], i32)
        idx = [sb(f"idx{v}", [TB, NS], i32) for v in range(2)]
        e_sb = [sb(f"e_sb{v}", [TB, NS * D]) for v in range(2)]
        eT = sb("eT", [128, NPAIR, TB])
        ege = sb("ege", [TB, NS, D])
        var1 = sb("var1", [TB, NS])
        sd1 = sb("sd1", [TB, NS])
        rstd1 = sb("rstd1", [TB, NS])
        es_sb = [sb(f"es_sb{v}", [TB, NS, D]) for v in range(2)]
        en_sb = [sb(f"en_sb{v}", [JN, G, D]) for v in range(2)]
        m0 = [sb(f"m0_{v}", [128, 512]) for v in range(2)]
        m1 = [sb(f"m1_{v}", [128, 512]) for v in range(2)]
        sq = sb("sq", [E, 2, 512])
        ssq = sb("ssq", [E, 2, 16])
        sd2 = sb("sd2", [E, 2, 16])
        rstd2 = sb("rstd2", [E, 2, 16])
        T = sb("T", [E, G, TW])
        zs = [sb(f"zs{v}", [JP, G, W34]) for v in range(2)]
        zb = [sb(f"zb{v}", [TB, P, W34]) for v in range(2)]
        cz = sb("cz", [TB, 5 * 128])
        xt = sb("xt", [128, 5, TB])
        bn6 = sb("bn6", [TB, 6])
        mv = sb("mv", [TB, 2])
        sd3 = sb("sd3", [TB, 1])
        rstd3 = sb("rstd3", [TB, 1])
        z_sb = sb("z_sb", [TB, DIMS])
        hT = sb("hT", [128, 3, 2, TB])
        h1T = sb("h1T", [128, 4, 2 * TB])
        h2T = sb("h2T", [128, 2, 2 * TB])
        y_sb = sb("y_sb", [1, B])

        pA = ps("pA", [128, 2, 512])
        pM = ps("pM", [128, 512])
        pY = ps("pY", [128, 2, 512])
        pZ = ps("pZ", [128, 4, 256])
        pW = ps("pW", [128, 512])

        w_early = sem("w_early")
        w_dense = sem("w_dense")
        w_pairs = sem("w_pairs")
        w_late = sem("w_late")
        dt_in = [sem(f"dt_in{h}") for h in range(2)]
        ids_in = sem("ids_in")
        consts_ready = sem("consts_ready")
        prep_dve = sem("prep_dve")
        prep_pe = sem("prep_pe")
        late_dve = sem("late_dve")
        late_pe = sem("late_pe")
        x_raw = sem("x_raw")
        x_sq = sem("x_sq")
        x_ssq = sem("x_ssq")
        x_sd = sem("x_sd")
        x_rstd = sem("x_rstd")
        x_scaled = sem("x_scaled")
        x_tr = sem("x_tr")
        x_out = sem("x_out")
        prep_pool = sem("prep_pool")
        consts_chain = sem("consts_chain")
        sp_step = sem("sp_step")
        pool_step = sem("pool_step")
        dve_step = sem("dve_step")
        idx_ready = sem("idx_ready")
        gathered = [sem(f"gathered{v}") for v in range(2)]
        tr_full = sem("tr_full")
        et_ready = sem("et_ready")
        gram_full = sem("gram_full")
        ege_ready = sem("ege_ready")
        var1_ready = sem("var1_ready")
        sd1_ready = sem("sd1_ready")
        scaled = sem("scaled")
        es_stored = [sem(f"es_stored{v}") for v in range(2)]
        en_loaded = [sem(f"en_loaded{v}") for v in range(2)]
        mix_full = sem("mix_full")
        m_ready = sem("m_ready")
        y_full = sem("y_full")
        sq_ready = sem("sq_ready")
        ssq_ready = sem("ssq_ready")
        sd2_ready = sem("sd2_ready")
        rstd2_ready = sem("rstd2_ready")
        t_ready = sem("t_ready")
        xcol_ready = sem("xcol_ready")
        z_full = sem("z_full")
        zs_act = sem("zs_act")
        zs_dve = sem("zs_dve")
        zs_stored = [sem(f"zs_stored{v}") for v in range(2)]
        zb_loaded = [sem(f"zb_loaded{v}") for v in range(2)]
        cz_dve = sem("cz_dve")
        cz_act = sem("cz_act")
        pair_full = sem("pair_full")
        xt_ready = sem("xt_ready")
        out_full = sem("out_full")
        bn_ready = sem("bn_ready")
        ln3_ready = sem("ln3_ready")
        sd3_ready = sem("sd3_ready")
        z_ready = sem("z_ready")
        zt_full = sem("zt_full")
        hT_ready = sem("hT_ready")
        h1_full = sem("h1_full")
        h1_ready = sem("h1_ready")
        h2_full = sem("h2_full")
        h2_ready = sem("h2_ready")
        top_full = sem("top_full")
        y_ready = sem("y_ready")
        y_stored = sem("y_stored")

        block = ctx.enter_context(nc.Block())

        def exists(t):
            return not isinstance(t, int) or 0 <= t < NT

        def is_tile(t, k):
            return isinstance(t, int) and t == k

        def later(n):
            return not isinstance(n, int) or n > 0

        def tiles(eng, tile, late=None):
            tile(-1, 1)
            if late:
                late()
            for i in (0, 1):
                tile(i, 0)
                tile(i, 1)
            with eng.Fori(2, NT // 2 - 1) as i:
                tile(i, 0)
                tile(i, 1)
            for i in (NT // 2 - 1, NT // 2):
                tile(i, 0)
                tile(i, 1)
            tile(NT // 2 + 1, 0)

        def rects(v, size):
            base = zb[v][:, 0:1, 0:1]
            free = [[2 * size * (W34 + 1), P // (2 * size)]] + ([[W34, size], [1, size]] if size > 1 else [])
            return bass.AP(tensor=base.tensor, offset=base.offset + size * W34, ap=[base.ap[0]] + free)

        early_dmas = [
            (ws[:, :], Ws), (vecs[:, 2:3], gs), (lhs0[D:D + 1, :], bs), (lhs1[0:1, :], bs),
            (wsi4[0:NS, :], WsiT), (wsi4[NS:2 * NS, :], WsiT), (wsi4[2 * NS:3 * NS, :], WsiT),
            (wsi4[3 * NS:4 * NS, :], WsiT),
        ]
        dense_dmas = [(wd[:, :, :], WdT.rearrange("(k p) e -> p k e", p=128)), (vecs[:, 0:1], gd), (vecs[:, 1:2], bd)]
        pairs_dmas = [(gb[:, 0:1], gsi), (gb[:, 1:2], bsi), (selT_sb[:, :, :], selT), (sel_sb[:, :, :, :], sel),
                      (isx_sb[:, :], isx)]
        late_dmas = [
            (wl[:, 0:4, :], WlT[0:512, :].rearrange("(k p) m -> p k m", p=128)),
            (wl[N_EXT:K4, 4, :], WlT[512:528, :]),
            (gl_sb[:, :], glc), (bl_sb[:, :], blc),
            (w1[:, 0:3, :], W1[0:DIMS, :].rearrange("(k p) m -> p k m", p=128)),
            (w1[:, 3:5, :], W1[OUT_LN:OUT_LN + KD, :].rearrange("(k p) m -> p k m", p=128)),
            (w2[:, :, :], W2.rearrange("(k p) m -> p k m", p=128)),
            (w3[:, :], W3c), (b1[:, :], b1c), (b2[:, :], b2c),
        ]
        W_EARLY, W_DENSE, W_PAIRS, W_LATE = (16 * len(dmas) for dmas in (early_dmas, dense_dmas, pairs_dmas, late_dmas))
        XC = B // 512

        def x_bank(c):
            return (pY if c < 2 else pA)[:, c % 2, :]

        def xt_bank(c):
            return pW if c % 2 else pM

        def first_bank(m):
            return (pW[:, :], pA[:, 1, :], pA[:, 0, :], pW[:, :])[m][:, 0:2 * TB]

        @block.sync
        def _(sp):
            sp.dma_start(idx_all[:, :, :], ids.rearrange("(t p) n -> p t n", p=TB)).then_inc(ids_in, 16)
            sp.wait_ge(consts_ready, 1)
            for dst, src in early_dmas:
                sp.dma_start(dst, src).then_inc(w_early, 16)
            for dst, src in dense_dmas:
                sp.dma_start(dst, src).then_inc(w_dense, 16)
            for h in range(2):
                half = slice(B // 2 * h, B // 2 * (h + 1))
                sp.dma_start(dt_all[:, :, half], dT[:, half].rearrange("(k p) b -> p k b", p=128))\
                    .then_inc(dt_in[h], 16)
            for dst, src in pairs_dmas:
                sp.dma_start(dst, src).then_inc(w_pairs, 16)
            for dst, src in late_dmas:
                sp.dma_start(dst, src).then_inc(w_late, 16)

            def tile(i, u):
                t = 2 * i + u
                v = 1 - u
                if exists(t - 1):
                    sp.wait_ge(zs_act, 32 * t)
                    sp.wait_ge(zs_dve, 32 * t)
                    sp.sem_inc(sp_step, 1)
                    sp.dma_start(z_dram[bass.ds(t - 1, 1)].rearrange("o g j p q -> (o j p) g q"),
                                 zs[v][:, :, :]).then_inc(zs_stored[v], 16)
                    sp.wait_ge(zs_stored[v], 16 * (i + u))
                    sp.sem_inc(sp_step, 1)
                    if later(t - 2):
                        sp.wait_ge(cz_dve, 7 * (t - 2))
                        sp.sem_inc(sp_step, 1)
                        sp.wait_ge(cz_act, 2 * (t - 2))
                    sp.sem_inc(sp_step, 1)
                    sp.dma_start(zb[v][:, :, :],
                                 z_dram[bass.ds(t - 1, 1)].rearrange("o g j p q -> (o g j) p q"))\
                      .then_inc(zb_loaded[v], 16)
                if exists(t + 1):
                    for h in range(2):
                        half = slice(NS // 2 * h, NS // 2 * (h + 1))
                        sp.wait_ge(scaled, 2 * (t + 1) + h + 1)
                        sp.sem_inc(sp_step, 1)
                        sp.dma_start(e_dram[bass.ds(t + 1, 1)].rearrange("o (b n) d -> (o b) n d", n=NS)[:, half, :],
                                     es_sb[v][:, half, :]).then_inc(es_stored[v], 16)
                    sp.wait_ge(es_stored[v], 32 * (i + u + 1))
                    sp.sem_inc(sp_step, 1)
                    if later(4 * t):
                        sp.wait_ge(mix_full, 4 * t)
                    sp.sem_inc(sp_step, 1)
                    sp.dma_start(en_sb[v][:, :, :],
                                 e_dram[bass.ds(t + 1, 1)].rearrange("o (g k) d -> (o k) g d", k=JN))\
                      .then_inc(en_loaded[v], 16)

            tiles(sp, tile)
            sp.wait_ge(y_ready, NT // 2)
            sp.dma_start(y_out.rearrange("b o -> o b"), y_sb[:, :]).then_inc(y_stored, 16)
            sp.wait_ge(y_stored, 16)

        @block.gpsimd
        def _(pool):
            nc.gpsimd.memset(ident[:, :], 0.0).then_inc(prep_pool, 1)
            nc.gpsimd.memset(blockmask[:, :], 1.0).then_inc(prep_pool, 1)
            pool.wait_ge(prep_pool, 2)
            nc.gpsimd.affine_select(out=ident[:, :], in_=ident[:, :], compare_op=ALU.not_equal, fill=1.0,
                                    base=0, pattern=[[-1, 128]], channel_multiplier=1).then_inc(prep_pool, 1)
            nc.gpsimd.affine_select(out=blockmask[:, :], in_=blockmask[:, :], compare_op=ALU.is_ge, fill=0.0,
                                    base=0, pattern=[[-NS, J]], channel_multiplier=1).then_inc(prep_pool, 1)
            pool.wait_ge(prep_pool, 4)
            nc.gpsimd.affine_select(out=blockmask[:, :], in_=blockmask[:, :], compare_op=ALU.is_ge, fill=0.0,
                                    base=NS - 1, pattern=[[NS, J]], channel_multiplier=-1).then_inc(prep_pool, 1)
            pool.wait_ge(ids_in, 16)

            def gather(i, v):
                t = 2 * i + v
                if later(16 * NS * i):
                    pool.wait_ge(gathered[v], 16 * NS * i)
                nc.gpsimd.tensor_copy(idx[v][:, :], idx_all[:, bass.ds(t, 1), :].rearrange("p o n -> p (o n)"))\
                  .then_inc(idx_ready, 1)
                pool.wait_ge(idx_ready, t + 1)
                if later(2 * (t - 1)):
                    pool.wait_ge(scaled, 2 * (t - 1))
                pool.sem_inc(pool_step, 1)
                for n in range(NS):
                    pool.indirect_dma_start(
                        out=e_sb[v][:, n * D:(n + 1) * D], out_offset=None, in_=tables[n],
                        in_offset=bass.IndirectOffsetOnAxis(ap=idx[v][:, n:n + 1], axis=0))\
                        .then_inc(gathered[v], 16)

            gather(0, 0)
            gather(0, 1)
            with pool.Fori(1, NT // 2) as i:
                gather(i, 0)
                gather(i, 1)

        @block.tensor
        def _(pe):
            mm = nc.tensor.matmul
            pe.wait_ge(w_early, W_EARLY)
            pe.wait_ge(consts_ready, 2)
            pe.wait_ge(prep_pool, 5)
            mm(pW[:, 0:D], avg[:, :], ws[:, :], start=True, stop=True).then_inc(prep_pe, 1)
            pe.wait_ge(prep_dve, 1)
            mm(pM[:, 0:128], ones[0:JN, :], mixw[:, :, :].rearrange("k j p -> k (j p)"), start=True, stop=True)\
                .then_inc(prep_pe, 1)
            pe.wait_ge(prep_dve, 2)
            wsc_flat = wsc2[:, :, :].rearrange("e a d -> e (a d)")
            mm(pZ[:, 0, 0:128], wsc_flat, wsc_flat, start=True, stop=True)
            nc.tensor.transpose(pZ[:, 2, 0:128], wscg2[:, :, :].rearrange("e a d -> e (a d)"), ident[:, :])\
              .then_inc(prep_pe, 1)
            pe.wait_ge(prep_dve, 3)
            for c in range(XC + 2):
                if c < XC:
                    pe.wait_ge(dt_in[2 * c // XC], 16)
                    for a in range(4):
                        t = 4 * c + a
                        for k in range(2):
                            last = mm(x_bank(c)[:, E * a:E * (a + 1)], dt_all[:, k, TB * t:TB * (t + 1)], wd[:, k, :],
                                      start=(k == 0), stop=(k == 1))
                    last.then_inc(x_raw, 1)
                if c >= 2:
                    pe.wait_ge(x_scaled, c - 1)
                    if c == 2:
                        pe.wait_ge(prep_dve, 4)
                    if c >= 4:
                        pe.wait_ge(x_out, c - 3)
                    for a in range(4):
                        last = nc.tensor.transpose(xt_bank(c)[:, TB * a:TB * (a + 1)], xr[:, c % 2, a, :], ident[:, :])
                    last.then_inc(x_tr, 1)

            pe.wait_ge(w_pairs, W_PAIRS)
            pe.wait_ge(late_dve, 1)
            pe.wait_ge(x_out, XC)
            for k in range(5):
                for h in range(2):
                    last = mm(pM[:, 4 * k + 2 * h:4 * k + 2 * h + 2], selT_sb[:, h, 128 * k:128 * (k + 1)],
                              gb[:, :], start=True, stop=True)
            last.then_inc(late_pe, 1)

            def late():
                for t in range(NT):
                    last = mm(pW[:, t:t + 1], x_all[:, TB * t:TB * (t + 1)], ones[:, 0:1], start=True, stop=True)
                last.then_inc(late_pe, 1)
                pe.wait_ge(w_late, W_LATE)
                pe.wait_ge(late_dve, 2)
                for k in range(5):
                    rows = 128 if k < 4 else K4
                    last = mm(pZ[0:K4, 0:2, :], dext[0:rows, k, :], wl[0:rows, k, :], start=(k == 0), stop=(k == 4))
                last.then_inc(late_pe, 1)

            def tile(i, u):
                t = 2 * i + u
                s = t + 1
                v = 1 - u

                def z_fill(c, f):
                    tz, c1 = (t, c - 1) if c else (t - 1, CH - 1)
                    if not exists(tz):
                        return
                    pe.wait_ge(t_ready, 8 * tz + 2 * c1 + f + 1)
                    if f == 0:
                        pe.wait_ge(xcol_ready, 4 * tz + c1 + 1)
                    if later(32 * tz + 8 * c1 + 4 * f):
                        pe.wait_ge(zs_act, 32 * tz + 8 * c1 + 4 * f)
                        pe.wait_ge(zs_dve, 32 * tz + 8 * c1 + 4 * f)
                    for a in range(4):
                        g = GC * c1 + 2 * a + f
                        last = mm(pZ[:, a, 0:TW], T[:, g, 0:JP], T[:, g, :], start=True, stop=True)
                    last.then_inc(z_full, 1)

                def ln1_transpose(s, w, si, q):
                    if not exists(s):
                        return
                    if q == 0:
                        pe.wait_ge(gathered[w], 16 * NS * (si + 1))
                    if q < 2:
                        if later(4 * s):
                            pe.wait_ge(ege_ready, 4 * s)
                        else:
                            pe.wait_ge(x_scaled, XC)
                            pe.wait_ge(prep_dve, 4)
                        if later(s - 2):
                            pe.wait_ge(xt_ready, s - 2)
                    else:
                        pe.wait_ge(et_ready, 4 * s + q - 1)
                    for a in range(4 * q, min(4 * q + 4, NPAIR)):
                        last = nc.tensor.transpose(pA[:, q % 2, 128 * (a - 4 * q):128 * (a - 4 * q + 1)],
                                                   e_sb[w][:, 128 * a:128 * (a + 1)], ident[:, :])
                    last.then_inc(tr_full, 1)

                def ln1_gram(q):
                    if not exists(s):
                        return
                    if q < 2:
                        pe.wait_ge(et_ready, 4 * s + q + 3)
                    else:
                        pe.wait_ge(ege_ready, 4 * s + q - 1)
                    for a in range(4 * q, min(4 * q + 4, NPAIR)):
                        last = mm(pA[:, q % 2, 128 * (a - 4 * q):128 * (a - 4 * q + 1)], eT[:, a, :], gram[:, :],
                                  start=True, stop=True)
                    last.then_inc(gram_full, 1)

                def mix(t, n, c, w, ti):
                    if not exists(t):
                        return
                    if c == 0:
                        pe.wait_ge(en_loaded[w], 16 * (ti + 1))
                        if not later(t):
                            pe.wait_ge(late_dve, 3)
                    if later(2 * n):
                        pe.wait_ge(m_ready, 2 * n)
                    for k in range(4):
                        g = GC * c + 2 * k
                        last = mm(pM[:, 128 * k:128 * (k + 1)], en_sb[w][:, g:g + 2, :],
                                  mixw[:, :, :], start=True, stop=True)
                    last.then_inc(mix_full, 1)

                def project(c):
                    if not exists(t):
                        return
                    n = 4 * t + c
                    pe.wait_ge(m_ready, 2 * n + 2)
                    for h in range(2):
                        if later(2 * n + h - 1):
                            pe.wait_ge(t_ready, 2 * n + h - 1)
                        if h == 0:
                            mm(pY[:, 0, :], lhs0[0:D + 1, :], m0[c % 2][0:D + 1, :], start=True, stop=True)\
                                .then_inc(y_full, 1)
                        else:
                            mm(pY[:, 1, :], lhs1[:, :], m1[c % 2][:, :], start=True, stop=True)\
                                .then_inc(y_full, 1)

                def pairs():
                    if not exists(t - 1):
                        return
                    pe.wait_ge(cz_dve, 7 * t)
                    pe.wait_ge(cz_act, 2 * t)
                    if exists(s):
                        pe.wait_ge(ege_ready, 4 * (s + 1))
                    if u == 1 and exists(t - 3):
                        pe.wait_ge(h1_ready, 4 * (i - 1) + 3)
                    if u == 0 and exists(t - 4):
                        pe.wait_ge(h2_ready, 2 * (i - 1))
                    for k in range(5):
                        last = nc.tensor.transpose(pA[:, k // 4, 128 * (k % 4):128 * (k % 4 + 1)],
                                                   cz[:, 128 * k:128 * (k + 1)], ident[:, :])
                    last.then_inc(pair_full, 1)

                def wl_product(part):
                    if not exists(t - 1):
                        return
                    pe.wait_ge(xt_ready, t)
                    if u == 1 and exists(t - 3):
                        pe.wait_ge(h1_ready, 4 * (i - 1) + 3)
                    elif u == 0 and exists(t - 4):
                        pe.wait_ge(y_ready, i - 1)
                    elif exists(t - 2):
                        pe.wait_ge(hT_ready, 3 * (t - 1))
                    for k in part:
                        rows = 128 if k < 4 else K4
                        last = mm(pW[:, :], xt[0:rows, k, :], wlg[0:rows, k, :], start=(k == 0), stop=(k == 4))
                    if 4 in part:
                        last.then_inc(out_full, 1)

                def z_transpose():
                    if not exists(t - 2):
                        return
                    pe.wait_ge(z_ready, t - 1)
                    if u == 0 and exists(t - 4):
                        pe.wait_ge(h1_ready, 4 * (i - 1))
                    for k in range(3):
                        last = nc.tensor.transpose(pW[:, 128 * k:128 * (k + 1)], z_sb[:, 128 * k:128 * (k + 1)],
                                                   ident[:, :])
                    last.then_inc(zt_full, 1)

                def mlp_first(m):
                    t0 = t - 3 if u == 1 else t - 4
                    if u != (m < 3) or not exists(t0):
                        return
                    if m == 0:
                        pe.wait_ge(hT_ready, 3 * (t - 1))
                    elif m < 3:
                        if exists(s):
                            pe.wait_ge(ege_ready, 4 * (s + 1))
                    elif exists(t - 2):
                        pe.wait_ge(z_ready, t - 1)
                    else:
                        pe.wait_ge(h1_ready, 4 * (i - 2) + 1)
                    for k in range(5):
                        rhs = hT[:, k, :, :] if k < 3 else dt_all[:, k - 3, bass.ds(TB * t0, 2 * TB)]
                        last = mm(first_bank(m), w1[:, k, 128 * m:128 * (m + 1)], rhs,
                                  start=(k == 0), stop=(k == 4))
                    last.then_inc(h1_full, 1)

                def mlp_second(m, part):
                    if not (u == 0 and exists(t - 4)):
                        return
                    pe.wait_ge(h1_ready, 4 * (i - 1))
                    if exists(s):
                        pe.wait_ge(ege_ready, 4 * (s + 1))
                    for k in part:
                        last = mm(pA[:, m, 0:2 * TB], w2[:, k, 128 * m:128 * (m + 1)], h1T[:, k, :],
                                  start=(k == 0), stop=(k == 3))
                    if 3 in part:
                        last.then_inc(h2_full, 1)

                def mlp_third():
                    if not (u == 0 and exists(t - 4)):
                        return
                    pe.wait_ge(h2_ready, 2 * (i - 1))
                    if exists(t - 2):
                        pe.wait_ge(hT_ready, 3 * (t - 1))
                    for k in range(2):
                        last = mm(pW[0:1, 0:256], w3[:, k:k + 1], h2T[:, k, :], start=(k == 0), stop=(k == 1))
                    last.then_inc(top_full, 1)

                if is_tile(t, -1):
                    for q in range(4):
                        ln1_transpose(0, 0, 0, q)
                if is_tile(t, 0):
                    mix(0, 0, 0, 0, 0)
                for c in range(CH):
                    n = 4 * t + c
                    z_fill(c, 0)
                    if c == 3:
                        pairs()
                    project(c)
                    if c == 0:
                        if is_tile(t, 0):
                            for q in range(4):
                                ln1_transpose(1, 1, 0, q)
                        ln1_gram(0)
                        ln1_gram(1)
                    if c == 1:
                        mlp_first(0)
                        mlp_first(3)
                    if c == 2:
                        mlp_second(0, (2, 3))
                    if c == 3:
                        mlp_third()
                        if later(t + 1):
                            ln1_transpose(t + 2, u, i + 1, 0)
                            ln1_transpose(t + 2, u, i + 1, 1)
                        wl_product(range(4))
                    if c < 3:
                        mix(t, n + 1, c + 1, u, i)
                    elif not is_tile(s, 0):
                        mix(s, n + 1, 0, v, i + u)
                    z_fill(c, 1)
                    if c == 0:
                        ln1_gram(2)
                        ln1_gram(3)
                        if u == 1:
                            z_transpose()
                    if c == 1:
                        if u == 0:
                            z_transpose()
                        mlp_first(1)
                        mlp_second(0, (0, 1))
                    if c == 2:
                        mlp_first(2)
                        mlp_second(1, (0, 1, 2, 3))
                    if c == 3:
                        wl_product((4,))
                        if later(t + 1):
                            ln1_transpose(t + 2, u, i + 1, 2)
                            ln1_transpose(t + 2, u, i + 1, 3)

            tiles(pe, tile, late)

        @block.scalar
        def _(act):
            def copy(out, in_, **k):
                return nc.scalar.activation(out, in_, ACT.Copy, **k)

            act.wait_ge(w_dense, W_DENSE)
            act.wait_ge(consts_ready, 2)
            for c in range(XC + 1):
                if c < XC:
                    act.wait_ge(x_raw, c + 1)
                    if c >= 2:
                        act.wait_ge(x_ssq, c - 1)
                    nc.scalar.activation(xsq[:, c % 2, :, :].rearrange("b a e -> b (a e)"), x_bank(c), ACT.Square)\
                        .then_inc(x_sq, 1)
                    act.wait_ge(x_ssq, c + 1)
                    nc.scalar.activation(xsd[:, 4 * c:4 * c + 4], xss[:, 4 * c:4 * c + 4], ACT.Sqrt,
                                         bias=eps[:, 0:1], scale=1.0 / E).then_inc(x_sd, 1)
                if c >= 1:
                    act.wait_ge(x_tr, c)
                    nc.scalar.activation(x_all[:, 512 * (c - 1):512 * c], xt_bank(c - 1)[:, :], ACT.Identity,
                                         bias=vecs[:, 1:2], scale=vecs[:, 0:1]).then_inc(x_out, 1)

            def tile(i, u):
                t = 2 * i + u
                s = t + 1
                v = 1 - u

                def z_copy(c, f):
                    tz, c1, w = (t, c - 1, u) if c else (t - 1, CH - 1, v)
                    if not exists(tz):
                        return
                    if c1 == 0 and f == 0 and later(16 * i):
                        act.wait_ge(zs_stored[w], 16 * i)
                    act.wait_ge(z_full, 8 * tz + 2 * c1 + f + 1)
                    groups = slice(GC * c1 + f, GC * (c1 + 1), 2)
                    for j in range(2):
                        quad = slice(P * j, P * (j + 1))
                        copy(zs[w][quad, groups, 0:P], pZ[quad, :, quad]).then_inc(zs_act, 1)
                        copy(zs[w][quad, groups, P:W34], pZ[quad, :, JP + j:TW:J]).then_inc(zs_act, 1)

                def ln1_copy(s, q):
                    if not exists(s):
                        return
                    act.wait_ge(tr_full, 4 * s + q + 1)
                    if q == 0 and later(4 * s):
                        act.wait_ge(gram_full, 4 * s)
                    a, n = 4 * q, min(4, NPAIR - 4 * q)
                    copy(eT[:, a:a + n, :], pA[:, q % 2, 0:128 * n]).then_inc(et_ready, 1)

                def mixed(t, n, c):
                    if not exists(t):
                        return
                    act.wait_ge(mix_full, n + 1)
                    if later(2 * (n - 1)):
                        act.wait_ge(y_full, 2 * (n - 1))
                    copy(m0[c % 2][0:D, :], pM[0:D, :]).then_inc(m_ready, 1)
                    copy(m1[c % 2][D:128, :], pM[D:128, :]).then_inc(m_ready, 1)

                def x_columns(t, c):
                    if not exists(t):
                        return
                    if later(8 * t + 2 * c - 6):
                        act.wait_ge(z_full, 8 * t + 2 * c - 6)
                    copy(T[:, GC * c:GC * (c + 1), JP:JP + J],
                         x_all[:, bass.ds(TB * t + 32 * c, 32)].rearrange("e (g j) -> e g j", j=J))\
                        .then_inc(xcol_ready, 1)

                def z_features():
                    if not exists(t - 2):
                        return
                    act.wait_ge(zt_full, t - 1)
                    if later(4 * (i - 1)):
                        act.wait_ge(h1_full, 4 * (i - 1))
                    for k in range(3):
                        nc.scalar.activation(hT[:, k, u, :], pW[:, 128 * k:128 * (k + 1)], ACT.Identity,
                                             bias=bl_sb[:, k:k + 1], scale=gl_sb[:, k:k + 1]).then_inc(hT_ready, 1)

                def relu_first(m):
                    if u != (m < 3) or not exists(t - 3 if u == 1 else t - 4):
                        return
                    act.wait_ge(h1_full, 4 * (i - 1) + m + 1 if u == 1 else 4 * (i - 1))
                    if m == 0 and later(2 * (i - 1)):
                        act.wait_ge(h2_full, 2 * (i - 1))
                    nc.scalar.activation(h1T[:, m, :], first_bank(m), ACT.Relu,
                                         bias=b1[:, m:m + 1]).then_inc(h1_ready, 1)

                def relu_second(m):
                    if not (u == 0 and exists(t - 4)):
                        return
                    act.wait_ge(h2_full, 2 * (i - 2) + m + 1)
                    if m == 0 and later(i - 2):
                        act.wait_ge(top_full, i - 2)
                    nc.scalar.activation(h2T[:, m, :], pA[:, m, 0:2 * TB], ACT.Relu,
                                         bias=b2[:, m:m + 1]).then_inc(h2_ready, 1)

                if is_tile(t, -1):
                    for q in range(4):
                        ln1_copy(0, q)
                if is_tile(t, 0):
                    mixed(0, 0, 0)
                    x_columns(0, 0)
                for c in range(CH):
                    n = 4 * t + c
                    z_copy(c, 0)
                    if c == 3 and exists(t - 1):
                        act.wait_ge(pair_full, t)
                        if later(t - 1):
                            act.wait_ge(out_full, t - 1)
                        copy(xt[:, :, :].rearrange("p k b -> p (k b)"),
                             pA[:, :, :].rearrange("p h b -> p (h b)")[:, 0:5 * TB]).then_inc(xt_ready, 1)
                    if exists(t):
                        for h in range(2):
                            act.wait_ge(y_full, 2 * n + h + 1)
                            if later(2 * n + h - 1):
                                act.wait_ge(ssq_ready, 2 * n + h - 1)
                            nc.scalar.activation(sq[:, h, :], pY[:, h, :], ACT.Square).then_inc(sq_ready, 1)
                    if c == 3 and u == 0 and exists(t - 4):
                        act.wait_ge(top_full, i - 1)
                        copy(y_sb[:, bass.ds(TB * (t - 4), 2 * TB)], pW[0:1, 0:256]).then_inc(y_ready, 1)
                    if exists(t):
                        for h in range(2):
                            act.wait_ge(ssq_ready, 2 * n + h + 1)
                            if later(2 * n + h - 1):
                                act.wait_ge(rstd2_ready, 2 * n + h - 1)
                            nc.scalar.activation(sd2[:, h, :], ssq[:, h, :], ACT.Sqrt, bias=eps[:, 1:2])\
                                .then_inc(sd2_ready, 1)
                    if c == 0 and is_tile(t, 0):
                        for q in range(4):
                            ln1_copy(1, q)
                    if c == 1:
                        if exists(s):
                            act.wait_ge(var1_ready, 4 * s + 3)
                            nc.scalar.activation(sd1[:, :], var1[:, :], ACT.Sqrt, bias=eps[:, 0:1])\
                                .then_inc(sd1_ready, 1)
                        relu_first(0)
                        relu_first(3)
                    if c == 3 and later(t + 1):
                        ln1_copy(t + 2, 0)
                        ln1_copy(t + 2, 1)
                    if c == 2 and exists(t - 1):
                        act.wait_ge(zb_loaded[v], 16 * (i + u))
                        if later(t - 1):
                            act.wait_ge(pair_full, t - 1)
                        copy(cz[:, 0:256].rearrange("b (r c) -> b r c", c=16), zb[v][:, 16:32, 0:16]).then_inc(cz_act, 1)
                        copy(cz[:, 256:384].rearrange("b (s r c) -> b s r c", r=8, c=8), rects(v, 8)).then_inc(cz_act, 1)
                    z_copy(c, 1)
                    if c < 3:
                        mixed(t, n + 1, c + 1)
                    elif not is_tile(s, 0):
                        mixed(s, n + 1, 0)
                    if c == 3 and exists(t - 1):
                        act.wait_ge(ln3_ready, 2 * t - 1)
                        nc.scalar.activation(sd3[:, :], mv[:, 1:2], ACT.Sqrt, bias=eps[:, 0:1]).then_inc(sd3_ready, 1)
                    if c == 0 and u == 1:
                        z_features()
                    if c < 3:
                        x_columns(t, c + 1)
                    elif not is_tile(s, 0):
                        x_columns(s, 0)
                    if c == 1:
                        if u == 0:
                            z_features()
                        relu_first(1)
                    if c == 2:
                        relu_first(2)
                        relu_second(0)
                        relu_second(1)
                    if c == 3 and later(t + 1):
                        ln1_copy(t + 2, 2)
                        ln1_copy(t + 2, 3)

            def late():
                act.wait_ge(w_late, W_LATE)

            tiles(act, tile, late)

        @block.vector
        def _(dve):
            V = nc.vector
            chain = [0]

            def link(ins):
                chain[0] += 1
                ins.then_inc(consts_chain, 1)
                dve.wait_ge(consts_chain, chain[0])

            V.memset(lhs1[0:D, :], 0.0)
            link(V.memset(wl[0:64, 4, :], 0.0))
            V.memset(eps[:, 0:1], EPS).then_inc(consts_ready, 1)
            V.memset(ones[:, :], 1.0)
            V.memset(gram[:, :], 0.0)
            V.memset(eps[:, 1:2], P * EPS)
            link(V.memset(cz[:, 512:640], 0.0))
            V.memset(avg[:, :], 1.0 / E).then_inc(consts_ready, 1)
            dve.wait_ge(w_early, W_EARLY)
            dve.wait_ge(prep_pool, 5)
            link(V.tensor_reduce(wsisum[:, :], wsi4[:, :], X, ALU.add))
            link(V.tensor_scalar(wsisum[:, :], wsisum[:, :], -1.0 / P, None, ALU.mult))
            link(V.tensor_scalar(wsi4[:, :], wsi4[:, :], wsisum[:, 0:1], None, ALU.add))
            for j in range(J):
                ins = V.tensor_scalar(mixw[:, j, :], wsi4[:, :], blockmask[:, j:j + 1], None, ALU.mult)
            ins.then_inc(prep_dve, 1)
            dve.wait_ge(prep_pe, 1)
            V.tensor_tensor(wsc2[:, 0, :], ws[:, :], pW[:, 0:D], ALU.subtract)
            link(V.tensor_tensor(wsc2[:, 1, :], ws[:, :], pW[:, 0:D], ALU.subtract))
            V.tensor_scalar(wscg2[:, :, :], wsc2[:, :, :], vecs[:, 2:3], None, ALU.mult).then_inc(prep_dve, 1)
            dve.wait_ge(w_dense, W_DENSE)
            link(V.tensor_reduce(wdsum[:, :], wd[:, :, :], X, ALU.add))
            link(V.tensor_scalar(wdsum[:, :], wdsum[:, :], -1.0 / E, None, ALU.mult))
            V.tensor_scalar(wd[:, 0, :], wd[:, 0, :], wdsum[:, 0:1], None, ALU.add)
            V.tensor_scalar(wd[:, 1, :], wd[:, 1, :], wdsum[:, 1:2], None, ALU.add).then_inc(prep_dve, 1)
            dve.wait_ge(prep_pe, 3)
            for h in range(2):
                q = slice(D * h, D * (h + 1))
                V.tensor_scalar(gram[q, q], pZ[q, 0, q], 1.0 / E, None, ALU.mult)
            V.tensor_copy(lhs0[0:D, :], pZ[0:D, 2, 0:128])
            V.tensor_copy(lhs1[D:128, :], pZ[D:128, 2, 0:128])
            for w in range(2):
                V.memset(m1[w][0:D, :], 0.0)
            link(V.memset(T[:, :, JP + J:TW], 1.0))
            for w in range(2):
                V.tensor_copy(m0[w][D:D + 1, :].rearrange("o (r c) -> o r c", c=128),
                              pM[D:D + 1, 0:128].unsqueeze(1).to_broadcast([1, 4, 128]))
                ins = V.tensor_copy(m1[w][0:1, :].rearrange("o (r c) -> o r c", c=128),
                                    pM[0:1, 0:128].unsqueeze(1).to_broadcast([1, 4, 128]))
            ins.then_inc(prep_dve, 1)
            for c in range(XC):
                dve.wait_ge(x_sq, c + 1)
                V.tensor_reduce(xss[:, 4 * c:4 * c + 4], xsq[:, c % 2, :, :], X, ALU.add).then_inc(x_ssq, 1)
                dve.wait_ge(x_sd, c + 1)
                V.reciprocal(xrstd[:, 4 * c:4 * c + 4], xsd[:, 4 * c:4 * c + 4]).then_inc(x_rstd, 1)
                dve.wait_ge(x_rstd, c + 1)
                if c >= 2:
                    dve.wait_ge(x_tr, c - 1)
                V.tensor_tensor(xr[:, c % 2, :, :], x_bank(c).rearrange("b (a e) -> b a e", e=E),
                                xrstd[:, 4 * c:4 * c + 4].unsqueeze(2).to_broadcast([TB, 4, E]), ALU.mult)\
                    .then_inc(x_scaled, 1)
            dve.wait_ge(w_pairs, W_PAIRS)
            V.tensor_scalar(gb[:, 0:1], gb[:, 0:1], float(P) ** 0.5, None, ALU.mult).then_inc(late_dve, 1)
            link(V.memset(dext[:, :, :], 0.0))
            V.memset(cz[:, 512 + P + 1:512 + P + 2], 1.0)
            dve.wait_ge(late_pe, 1)
            link(V.tensor_copy(pv[:, :, :], pM[:, 0:20].rearrange("p (k a) -> p k a", a=4)))
            gp, bp, gq, bq = (pv[:, :, a] for a in range(4))
            V.tensor_tensor(pg[:, 3, :], gq, isx_sb[:, :], ALU.add)
            V.tensor_tensor(pg[:, 1, :], gp, bq, ALU.mult)
            link(V.tensor_tensor(pg[:, 2, :], gq, bp, ALU.mult))
            V.tensor_tensor(pg[:, 0, :], gp, pg[:, 3, :], ALU.mult)
            V.tensor_tensor(dext[:, :, P], isx_sb[:, :], bp, ALU.mult)
            V.scalar_tensor_tensor(dext[:, :, P + 1], bp, float(E), bq, ALU.mult, ALU.mult)
            for k in range(5):
                ins = V.tensor_scalar(dtmp[:, k, :], sel_sb[:, 0, k, :], pg[:, 1, k:k + 1], None, ALU.mult)
            link(ins)
            for k in range(5):
                ins = V.scalar_tensor_tensor(dext[:, k, 0:P], sel_sb[:, 1, k, :], pg[:, 2, k:k + 1],
                                             dtmp[:, k, :], ALU.mult, ALU.add)
            ins.then_inc(late_dve, 1)

            def late():
                dve.wait_ge(late_pe, 2)
                V.tensor_copy(sx_all[:, :], pW[:, 0:NT])
                dve.wait_ge(w_late, W_LATE)
                for k in range(4):
                    V.tensor_scalar(wlg[:, k, :], wl[:, k, :], pg[:, 0, k:k + 1], None, ALU.mult)
                dve.wait_ge(late_pe, 3)
                V.scalar_tensor_tensor(wlg[0:K4, 4, :], wl[0:K4, 4, :], pg[0:K4, 0, 4:5],
                                       pZ[0:K4, 0:2, :].rearrange("p a m -> p (a m)"), ALU.mult, ALU.add)\
                    .then_inc(late_dve, 1)

            def tile(i, u):
                t = 2 * i + u
                s = t + 1
                v = 1 - u

                def z_copy(c, f):
                    tz, c1, w = (t, c - 1, u) if c else (t - 1, CH - 1, v)
                    if not exists(tz):
                        return
                    if c1 == 0 and f == 0 and later(16 * i):
                        dve.wait_ge(zs_stored[w], 16 * i)
                    dve.wait_ge(z_full, 8 * tz + 2 * c1 + f + 1)
                    groups = slice(GC * c1 + f, GC * (c1 + 1), 2)
                    for j in range(2, 4):
                        quad = slice(P * j, P * (j + 1))
                        V.tensor_copy(zs[w][quad, groups, 0:P], pZ[quad, :, quad]).then_inc(zs_dve, 1)
                        V.tensor_copy(zs[w][quad, groups, P:W34], pZ[quad, :, JP + j:TW:J]).then_inc(zs_dve, 1)

                def ln1_product(q):
                    if not exists(s):
                        return
                    if q == 0:
                        dve.wait_ge(gathered[v], 16 * NS * (i + u + 1))
                    dve.wait_ge(gram_full, 4 * s + q + 1)
                    a, n = 512 * q, min(512, NS * D - 512 * q)
                    flat = ege[:, :, :].rearrange("b n d -> b (n d)")
                    V.tensor_tensor(flat[:, a:a + n], pA[:, q % 2, 0:n], e_sb[v][:, a:a + n], ALU.mult)\
                        .then_inc(ege_ready, 1)

                def ln1_sum(h):
                    if not exists(s):
                        return
                    half = slice(NS // 2 * h, NS // 2 * (h + 1))
                    dve.wait_ge(ege_ready, 4 * s + 4)
                    V.tensor_reduce(var1[:, half], ege[:, half, :], X, ALU.add).then_inc(var1_ready, 1)

                def ln1_guard():
                    if not exists(s):
                        return
                    dve.wait_ge(var1_ready, 4 * s + 2)
                    V.tensor_scalar(var1[:, :], var1[:, :], 0.0, None, ALU.max).then_inc(var1_ready, 1)

                def ln1_scale(h):
                    if not exists(s):
                        return
                    if h == 0:
                        dve.wait_ge(sd1_ready, s + 1)
                        V.reciprocal(rstd1[:, :], sd1[:, :]).then_inc(var1_ready, 1)
                        dve.wait_ge(var1_ready, 4 * s + 4)
                        if later(32 * (i + u)):
                            dve.wait_ge(es_stored[v], 32 * (i + u))
                    half = slice(NS // 2 * h, NS // 2 * (h + 1))
                    V.tensor_tensor(es_sb[v][:, half, :],
                                    e_sb[v][:, :].rearrange("b (n d) -> b n d", d=D)[:, half, :],
                                    rstd1[:, half].unsqueeze(2).to_broadcast([TB, NS // 2, D]), ALU.mult)\
                        .then_inc(scaled, 1)

                def compact():
                    if not exists(t - 1):
                        return
                    dve.wait_ge(zb_loaded[v], 16 * (i + u))
                    if later(t - 1):
                        dve.wait_ge(pair_full, t - 1)
                    V.tensor_copy(cz[:, 384:448].rearrange("b (s r c) -> b s r c", r=4, c=4), rects(v, 4)).then_inc(cz_dve, 1)
                    V.tensor_copy(cz[:, 448:480].rearrange("b (s r c) -> b s r c", r=2, c=2), rects(v, 2)).then_inc(cz_dve, 1)
                    V.tensor_copy(cz[:, 480:496], rects(v, 1)).then_inc(cz_dve, 1)
                    V.tensor_copy(cz[:, 496:512], zb[v][:, 0:16, P]).then_inc(cz_dve, 1)
                    V.tensor_copy(cz[:, 512 + N_EXT:512 + K4], zb[v][:, 16:32, P]).then_inc(cz_dve, 1)
                    V.tensor_copy(cz[:, 512:512 + P], zb[v][:, :, P + 1]).then_inc(cz_dve, 1)
                    V.tensor_copy(cz[:, 512 + P:512 + P + 1], sx_all[:, bass.ds(t - 1, 1)]).then_inc(cz_dve, 1)

                def ln3_statistics():
                    if not exists(t - 1):
                        return
                    dve.wait_ge(out_full, t)
                    V.bn_stats(bn6[:, :], pW[:, :]).then_inc(bn_ready, 1)
                    dve.wait_ge(bn_ready, t)
                    dve.sem_inc(dve_step, 1)
                    V.bn_aggr(mv[:, :], bn6[:, :]).then_inc(ln3_ready, 1)

                def ln3_rows():
                    if not exists(t - 1):
                        return
                    dve.wait_ge(sd3_ready, t)
                    V.reciprocal(rstd3[:, :], sd3[:, :]).then_inc(ln3_ready, 1)
                    dve.wait_ge(ln3_ready, 2 * t)
                    if later(t - 1):
                        dve.wait_ge(zt_full, t - 1)
                    V.tensor_scalar(z_sb[:, :], pW[:, 0:DIMS], mv[:, 0:1], rstd3[:, 0:1], ALU.subtract, ALU.mult)\
                        .then_inc(z_ready, 1)

                def sum_squares(n, h):
                    if not exists(t):
                        return
                    dve.wait_ge(sq_ready, 2 * n + h + 1)
                    V.tensor_reduce(ssq[:, h, :], sq[:, h, :].rearrange("e (b p) -> e b p", p=P), X, ALU.add)\
                        .then_inc(ssq_ready, 1)

                def normalize(c, n, h):
                    if not exists(t):
                        return
                    dve.wait_ge(sd2_ready, 2 * n + h + 1)
                    V.reciprocal(rstd2[:, h, :], sd2[:, h, :]).then_inc(rstd2_ready, 1)
                    dve.wait_ge(rstd2_ready, 2 * n + h + 1)
                    if later(8 * t + 2 * c + h - 7):
                        dve.wait_ge(z_full, 8 * t + 2 * c + h - 7)
                    V.tensor_tensor(T[:, GC * c + h:GC * (c + 1):2, 0:JP].rearrange("e k (j p) -> e k j p", p=P),
                                    pY[:, h, :].rearrange("e (k j p) -> e k j p", j=J, p=P),
                                    rstd2[:, h, :].rearrange("e (k j) -> e k j", j=J).unsqueeze(3)
                                    .to_broadcast([E, 4, J, P]), ALU.mult).then_inc(t_ready, 1)

                for c in range(CH):
                    n = 4 * t + c
                    z_copy(c, 0)
                    if c == 1:
                        ln1_sum(1)
                        ln1_guard()
                    if c == 2:
                        ln1_scale(1)
                    sum_squares(n, 0)
                    sum_squares(n, 1)
                    normalize(c, n, 0)
                    if c == 0:
                        if is_tile(t, 0):
                            z_copy(0, 1)
                            normalize(0, 0, 1)
                        ln1_product(0)
                        ln1_product(1)
                        if not is_tile(t, 0):
                            z_copy(0, 1)
                            normalize(0, n, 1)
                        ln1_product(2)
                        ln1_product(3)
                        ln1_sum(0)
                    if c == 1:
                        if u == 1:
                            normalize(1, n, 1)
                        z_copy(1, 1)
                        if u == 0:
                            normalize(1, n, 1)
                        ln1_scale(0)
                    if c == 2:
                        z_copy(2, 1)
                        compact()
                        normalize(2, n, 1)
                    if c == 3:
                        normalize(3, n, 1)
                        z_copy(3, 1)
                        ln3_statistics()
                        ln3_rows()

            tiles(dve, tile, late)


def kernel(**inputs):
    import concourse.bacc as bacc
    from concourse.bass_utils import run_bass_kernel_spmd as run

    nc = bacc.Bacc("TRN2", target_bir_lowering=False, num_devices=1)
    blocks = pair_blocks()
    f32 = np.float32
    selT = np.zeros((P, 2, 5 * 128), f32)
    sel = np.zeros((128, 2, 5, P), f32)
    isx = np.zeros((128, 5), f32)
    columns = []
    for k, rows in enumerate(blocks):
        for r, pair in enumerate(rows):
            if pair is None:
                continue
            p, q = pair
            columns.append(p * (p + 1) // 2 + q + 1)
            for h, c in ((0, p), (1, q)):
                if c >= 0:
                    selT[c, h, 128 * k + r] = 1
                    sel[r, h, k, c] = 1
            isx[r, k] = q < 0
    a = {k: np.asarray(v) for k, v in inputs.items()}
    col = lambda x: x.reshape(-1, 1)
    blocked = lambda x: np.ascontiguousarray(x.reshape(-1, 128).T)
    arrays = {
        "ids": a["ids"],
        **{f"tbl_{n}": a[f"tbl_{n}"] for n in range(NS)},
        "dT": a["r_dense_t"].T, "WdT": a["L0_rec_Wd"].T, "gd": col(a["L0_rec_gd"]), "bd": col(a["L0_rec_bd"]),
        "Ws": a["L0_rec_Ws"], "gs": col(a["L0_rec_gs"]), "bs": a["L0_rec_bs"].reshape(1, -1),
        "WsiT": a["L0_rec_Wsi"].T, "gsi": col(a["L0_rec_gsi"]), "bsi": col(a["L0_rec_bsi"]),
        "WlT": a["L0_rec_Wl"].T[columns], "glc": blocked(a["L0_rec_gl"][:DIMS]),
        "blc": blocked(a["L0_rec_bl"][:DIMS]),
        "W1": a["W_top1"], "b1c": blocked(a["b_top1"]), "W2": a["W_top2"], "b2c": blocked(a["b_top2"]),
        "W3c": blocked(a["W_top3"]), "selT": selT, "sel": sel, "isx": isx,
    }
    arrays = {k: np.ascontiguousarray(v) for k, v in arrays.items()}
    aps = {k: nc.dram_tensor(k, v.shape, mybir.dt.from_np(v.dtype), kind="ExternalInput").ap()
           for k, v in arrays.items()}
    tables = [aps.pop(f"tbl_{n}") for n in range(NS)]
    y = nc.dram_tensor("y", (B, 1), mybir.dt.float32, kind="ExternalOutput").ap()
    e_dram = nc.dram_tensor("e_dram", (NT, TB * NS, D), mybir.dt.float32, kind="Internal").ap()
    z_dram = nc.dram_tensor("z_dram", (NT, G, J, P, W34), mybir.dt.float32, kind="Internal").ap()
    build(nc, tables=tables, y_out=y, e_dram=e_dram, z_dram=z_dram, **aps)
    r = run(nc, [arrays], core_ids=[0])
    return r.results[0]["y"]
```

```python
import numpy as np
import concourse.bass as bass
from concourse import mybir
from contextlib import ExitStack

B, NS, D, E, P, KD = 2048, 26, 64, 128, 32, 256
OUT_LN, DIMS, H1, H2 = 512, 384, 512, 256
TB = 128
NT = B // TB
J = 4
G = TB // J
CH = 4
GC = G // CH
JN = J * NS
JP = J * P
W34 = P + 2
TW = J * W34
NPAIR = NS // 2
EPS = 1e-5
N_EXT = P + 2
K4 = N_EXT + P // 2
K4_REST = 64
WL_EARLY = [(k, 0) for k in range(4)] + [(k, 1) for k in range(5)]
WL_LATE = [(k, 2) for k in range(4)] + [(4, 0)]


def pair_blocks():
    blocks = [[(p, q) for p in range(16, 24) for q in range(16)],
              [(p, q) for p in range(24, 32) for q in range(16)],
              [(16 * s + 8 + r, 16 * s + c) for s in range(2) for r in range(8) for c in range(8)],
              [(8 * s + 4 + r, 8 * s + c) for s in range(4) for r in range(4) for c in range(4)]
              + [(4 * s + 2 + r, 4 * s + c) for s in range(8) for r in range(2) for c in range(2)]
              + [(2 * s + 1, 2 * s) for s in range(16)] + [(p, -1) for p in range(16)],
              [None] * N_EXT + [(p, -1) for p in range(16, 32)]]
    return blocks


def build(nc, ids, tables, dT, WdT, gd, bd, Ws, gs, bs, WsiT, gsi, bsi, WlT, glc, blc,
          W1, b1c, W2, b2c, W3c, selT, sel, isx, y_out, e_dram, z_dram):
    fp32 = mybir.dt.float32
    fp32r = mybir.dt.float32r
    i32 = mybir.dt.int32
    ALU = mybir.AluOpType
    ACT = mybir.ActivationFunctionType
    X = mybir.AxisListType.X

    ctx = ExitStack()
    with ctx:
        def sb(name, shape, dt=fp32):
            return ctx.enter_context(nc.sbuf_tensor(name, shape, dt))

        def ps(name, shape):
            return ctx.enter_context(nc.psum_tensor(name, shape, fp32))

        def sem(name):
            return ctx.enter_context(nc.semaphore(name))

        ident = sb("ident", [128, 128])
        ones = sb("ones", [128, 128])
        avg = sb("avg", [128, 128])
        eps = sb("eps", [128, 2])
        blockmask = sb("blockmask", [JN, J])
        ws = sb("ws", [E, D])
        wsc2 = sb("wsc2", [E, 2, D])
        wscg2 = sb("wscg2", [E, 2, D])
        gram = sb("gram", [128, 128])
        lhs0 = sb("lhs0", [128, E])
        lhs1 = sb("lhs1", [128, E])
        wsi4 = sb("wsi4", [JN, P])
        wsisum = sb("wsisum", [JN, 1])
        mixw = sb("mixw", [JN, J, P])
        wd = sb("wd", [128, 2, E])
        wdsum = sb("wdsum", [128, 2])
        wl = sb("wl", [128, 5, OUT_LN])
        wl_hi = sb("wl_hi", [128, 5, OUT_LN], fp32r)
        wl_lo = sb("wl_lo", [128, 5, OUT_LN], fp32r)
        selT_sb = sb("selT_sb", [2 * P, 5 * 128])
        sel_sb = sb("sel_sb", [128, 2, 5, P])
        isx_sb = sb("isx_sb", [128, 5])
        gb = sb("gb", [2 * P, 4])
        pv = sb("pv", [128, 5, 4])
        pg = sb("pg", [128, 4, 5])
        dext = sb("dext", [128, 5, K4])
        dtmp = sb("dtmp", [128, 5, P])
        vecs = sb("vecs", [128, 4])
        gl_sb = sb("gl_sb", [128, 3])
        bl_sb = sb("bl_sb", [128, 3])
        w1 = sb("w1", [128, 5, H1])
        w2 = sb("w2", [128, 4, H2])
        w3 = sb("w3", [128, 2])
        b1 = sb("b1", [128, 4])
        b2 = sb("b2", [128, 2])
        dt_all = sb("dt_all", [128, 2, B])
        xss = sb("xss", [TB, NT])
        xsd = sb("xsd", [TB, NT])
        xrstd = sb("xrstd", [TB, NT])
        x_all = sb("x_all", [E, B])
        sx_all = sb("sx_all", [TB, NT])
        idx_all = sb("idx_all", [TB, NT, NS], i32)
        idx = [sb(f"idx{v}", [TB, NS], i32) for v in range(2)]
        e_sb = [sb(f"e_sb{v}", [TB, NS * D]) for v in range(2)]
        eT = sb("eT", [128, NPAIR, TB])
        ege = sb("ege", [TB, NS, D])
        var1 = sb("var1", [TB, NS])
        sd1 = sb("sd1", [TB, NS])
        rstd1 = sb("rstd1", [TB, NS])
        es_sb = sb("es_sb", [TB, NS, D])
        en_sb = [sb(f"en_sb{v}", [JN, G, D]) for v in range(2)]
        m0_hi, m1_hi, m0_lo, m1_lo = (sb(name, [128, 512], fp32r) for name in ("m0_hi", "m1_hi", "m0_lo", "m1_lo"))
        lhs0_hi, lhs1_hi, lhs0_lo, lhs1_lo = (sb(name, [128, E], fp32r)
                                              for name in ("lhs0_hi", "lhs1_hi", "lhs0_lo", "lhs1_lo"))
        m1_rows = sb("m1_rows", [D, 128])
        sq = sb("sq", [E, 2, 512])
        ssq = sb("ssq", [E, 2, 16])
        sd2 = sb("sd2", [E, 2, 16])
        rstd2 = sb("rstd2", [E, 2, 16])
        T = sb("T", [E, G, TW])
        zs = [sb(f"zs{v}", [JP, G, W34]) for v in range(2)]
        zb = [sb(f"zb{v}", [TB, P, W34]) for v in range(2)]
        cz = sb("cz", [TB, 5 * 128])
        xt_hi = sb("xt_hi", [128, 5, TB], fp32r)
        xt_lo = sb("xt_lo", [128, 4, TB], fp32r)
        bn6 = sb("bn6", [TB, 6])
        mv = sb("mv", [TB, 2])
        sd3 = sb("sd3", [TB, 1])
        rstd3 = sb("rstd3", [TB, 1])
        z_sb = sb("z_sb", [TB, DIMS])
        hT = sb("hT", [128, 3, 2, TB])
        h1T = sb("h1T", [128, 4, 2 * TB])
        h2T = sb("h2T", [128, 2, 2 * TB])
        y_sb = sb("y_sb", [1, B])
        xsq = sq[:, :, :].rearrange("b h (a e) -> b h a e", e=E)
        xr = h1T[:, :, :].rearrange("b (h a) e -> b h (a e)", h=2).rearrange("b h (a e) -> b h a e", e=E)

        pA = ps("pA", [128, 2, 512])
        pM = ps("pM", [128, 512])
        pY = ps("pY", [128, 2, 512])
        pZ = ps("pZ", [128, 4, 256])
        pW = ps("pW", [128, 512])

        w_early = sem("w_early")
        w_dense = sem("w_dense")
        w_pairs = sem("w_pairs")
        w_late = sem("w_late")
        dt_in = [sem(f"dt_in{h}") for h in range(2)]
        ids_in = sem("ids_in")
        consts_ready = sem("consts_ready")
        prep_dve = sem("prep_dve")
        prep_pe = sem("prep_pe")
        late_dve = sem("late_dve")
        late_pe = sem("late_pe")
        wl_split = sem("wl_split")
        x_raw = sem("x_raw")
        x_sq = sem("x_sq")
        x_ssq = sem("x_ssq")
        x_sd = sem("x_sd")
        x_rstd = sem("x_rstd")
        x_scaled = sem("x_scaled")
        x_tr = sem("x_tr")
        x_out = sem("x_out")
        prep_pool = sem("prep_pool")
        consts_chain = sem("consts_chain")
        sp_step = sem("sp_step")
        pool_step = sem("pool_step")
        dve_step = sem("dve_step")
        idx_ready = sem("idx_ready")
        first_rows = [[sem(f"first_rows{v}_{q}") for q in range(4)] for v in range(2)]
        gathered = [sem(f"gathered{v}") for v in range(2)]
        tr_full = sem("tr_full")
        et_ready = sem("et_ready")
        gram_full = sem("gram_full")
        ege_ready = sem("ege_ready")
        var1_ready = sem("var1_ready")
        sd1_ready = sem("sd1_ready")
        scaled = sem("scaled")
        es_stored = [sem(f"es_stored{v}") for v in range(2)]
        en_loaded = [[sem(f"en_loaded{v}_{h}") for h in range(2)] for v in range(2)]
        mix_full = sem("mix_full")
        m_ready = sem("m_ready")
        m_rest = sem("m_rest")
        y_full = sem("y_full")
        sq_ready = sem("sq_ready")
        ssq_ready = sem("ssq_ready")
        sd2_ready = sem("sd2_ready")
        rstd2_ready = sem("rstd2_ready")
        t_ready = sem("t_ready")
        xcol_ready = sem("xcol_ready")
        z_full = sem("z_full")
        zs_ready = sem("zs_ready")
        zs_stored = [sem(f"zs_stored{v}") for v in range(2)]
        zb_loaded = [sem(f"zb_loaded{v}") for v in range(2)]
        cz_dve = sem("cz_dve")
        cz_act = sem("cz_act")
        pair_full = sem("pair_full")
        xt_ready = sem("xt_ready")
        xt_rest = sem("xt_rest")
        out_full = sem("out_full")
        bn_ready = sem("bn_ready")
        ln3_ready = sem("ln3_ready")
        sd3_ready = sem("sd3_ready")
        z_ready = sem("z_ready")
        zt_full = sem("zt_full")
        hT_ready = sem("hT_ready")
        h1_full = sem("h1_full")
        h1_ready = sem("h1_ready")
        h2_full = sem("h2_full")
        h2_ready = sem("h2_ready")
        top_full = sem("top_full")
        y_ready = sem("y_ready")
        y_stored = sem("y_stored")

        block = ctx.enter_context(nc.Block())

        def exists(t):
            return not isinstance(t, int) or 0 <= t < NT

        def is_tile(t, k):
            return isinstance(t, int) and t == k

        def later(n):
            return not isinstance(n, int) or n > 0

        def tiles(eng, tile, late=None):
            tile(-1, 1)
            if late:
                late()
            for i in (0, 1):
                tile(i, 0)
                tile(i, 1)
            with eng.Fori(2, NT // 2 - 1) as i:
                tile(i, 0)
                tile(i, 1)
            for i in (NT // 2 - 1, NT // 2):
                tile(i, 0)
                tile(i, 1)
            tile(NT // 2 + 1, 0)

        def rects(v, size):
            base = zb[v][:, 0:1, 0:1]
            free = [[2 * size * (W34 + 1), P // (2 * size)]] + ([[W34, size], [1, size]] if size > 1 else [])
            return bass.AP(tensor=base.tensor, offset=base.offset + size * W34, ap=[base.ap[0]] + free)

        early_dmas = [
            (ws[:, :], Ws), (vecs[:, 2:3], gs), (lhs0[D:D + 1, :], bs), (lhs1[0:1, :], bs),
            (wsi4[0:NS, :], WsiT), (wsi4[NS:2 * NS, :], WsiT), (wsi4[2 * NS:3 * NS, :], WsiT),
            (wsi4[3 * NS:4 * NS, :], WsiT),
        ]
        dense_dmas = [(wd[:, :, :], WdT.rearrange("(k p) e -> p k e", p=128)), (vecs[:, 0:1], gd), (vecs[:, 1:2], bd)]
        pairs_dmas = [(gb[0:P, 0:1], gsi), (gb[0:P, 1:2], bsi), (gb[P:2 * P, 2:3], gsi), (gb[P:2 * P, 3:4], bsi),
                      (selT_sb[:, :], selT), (sel_sb[:, :, :, :], sel), (isx_sb[:, :], isx)]
        late_dmas = [
            (wl[:, 0:4, :], WlT[0:512, :].rearrange("(k p) m -> p k m", p=128)),
            (wl[N_EXT:K4, 4, :], WlT[512:528, :]),
            (gl_sb[:, :], glc), (bl_sb[:, :], blc),
            (w1[:, 0:3, :], W1[0:DIMS, :].rearrange("(k p) m -> p k m", p=128)),
            (w1[:, 3:5, :], W1[OUT_LN:OUT_LN + KD, :].rearrange("(k p) m -> p k m", p=128)),
            (w2[:, :, :], W2.rearrange("(k p) m -> p k m", p=128)),
            (w3[:, :], W3c), (b1[:, :], b1c), (b2[:, :], b2c),
        ]
        W_EARLY, W_DENSE, W_PAIRS, W_LATE = (16 * len(dmas) for dmas in (early_dmas, dense_dmas, pairs_dmas, late_dmas))
        XC = B // 512

        def x_bank(c):
            return (pY if c < 2 else pA)[:, c % 2, :]

        def xt_bank(c):
            return pW if c % 2 else pM

        def first_bank(m):
            return (pW[:, :], pA[:, 1, :], pA[:, 0, :], pW[:, :])[m][:, 0:2 * TB]

        def last_bank(m):
            return (pY[:, 0, :], pY[:, 1, :], pM[:, :], pZ[:, 0:2, :].rearrange("p a b -> p (a b)"))[m][:, 0:2 * TB]

        @block.sync
        def _(sp):
            sp.dma_start(idx_all[:, :, :], ids.rearrange("(t p) n -> p t n", p=TB)).then_inc(ids_in, 16)
            sp.wait_ge(consts_ready, 1)
            for dst, src in early_dmas:
                sp.dma_start(dst, src).then_inc(w_early, 16)
            for dst, src in dense_dmas:
                sp.dma_start(dst, src).then_inc(w_dense, 16)
            for h in range(2):
                half = slice(B // 2 * h, B // 2 * (h + 1))
                sp.dma_start(dt_all[:, :, half], dT[:, half].rearrange("(k p) b -> p k b", p=128))\
                    .then_inc(dt_in[h], 16)
            for dst, src in pairs_dmas:
                sp.dma_start(dst, src).then_inc(w_pairs, 16)
            for dst, src in late_dmas:
                sp.dma_start(dst, src).then_inc(w_late, 16)

            def z_store(tz, w, h):
                sp.wait_ge(zs_ready, 8 * J * (2 * tz + h + 1))
                sp.sem_inc(sp_step, 1)
                half = slice(G // 2 * h, G // 2 * (h + 1))
                sp.dma_start(z_dram[bass.ds(tz, 1)].rearrange("o g j p q -> (o j p) g q")[:, half, :],
                             zs[w][:, half, :]).then_inc(zs_stored[w], 16)

            def tile(i, u):
                t = 2 * i + u
                v = 1 - u
                if exists(t - 1):
                    z_store(t - 1, v, 1)
                    sp.wait_ge(zs_stored[v], 32 * (i + u))
                    sp.sem_inc(sp_step, 1)
                    if later(t - 2):
                        sp.wait_ge(cz_dve, 7 * (t - 2))
                        sp.sem_inc(sp_step, 1)
                        sp.wait_ge(cz_act, 2 * (t - 2))
                    sp.sem_inc(sp_step, 1)
                    sp.dma_start(zb[v][:, :, :],
                                 z_dram[bass.ds(t - 1, 1)].rearrange("o g j p q -> (o g j) p q"))\
                      .then_inc(zb_loaded[v], 16)
                if exists(t + 1):
                    for h in range(2):
                        half = slice(NS // 2 * h, NS // 2 * (h + 1))
                        sp.wait_ge(scaled, 2 * (t + 1) + h + 1)
                        sp.sem_inc(sp_step, 1)
                        sp.dma_start(e_dram[bass.ds(t + 1, 1)].rearrange("o (b n) d -> (o b) n d", n=NS)[:, half, :],
                                     es_sb[:, half, :]).then_inc(es_stored[v], 16)
                    sp.wait_ge(es_stored[v], 32 * (i + u + 1))
                    sp.sem_inc(sp_step, 1)
                    if later(4 * t):
                        sp.wait_ge(mix_full, 4 * t)
                    sp.sem_inc(sp_step, 1)
                    for h in range(2):
                        half = slice(G // 2 * h, G // 2 * (h + 1))
                        sp.dma_start(en_sb[v][:, half, :],
                                     e_dram[bass.ds(t + 1, 1)].rearrange("o (g k) d -> (o k) g d", k=JN)[:, half, :])\
                            .then_inc(en_loaded[v][h], 16)
                if exists(t):
                    z_store(t, u, 0)

            tiles(sp, tile)
            sp.wait_ge(y_ready, NT // 2)
            sp.dma_start(y_out.rearrange("b o -> o b"), y_sb[:, :]).then_inc(y_stored, 16)
            sp.wait_ge(y_stored, 16)

        @block.gpsimd
        def _(pool):
            nc.gpsimd.memset(ident[:, :], 0.0).then_inc(prep_pool, 1)
            nc.gpsimd.memset(blockmask[:, :], 1.0).then_inc(prep_pool, 1)
            pool.wait_ge(prep_pool, 2)
            nc.gpsimd.affine_select(out=ident[:, :], in_=ident[:, :], compare_op=ALU.not_equal, fill=1.0,
                                    base=0, pattern=[[-1, 128]], channel_multiplier=1).then_inc(prep_pool, 1)
            nc.gpsimd.affine_select(out=blockmask[:, :], in_=blockmask[:, :], compare_op=ALU.is_ge, fill=0.0,
                                    base=0, pattern=[[-NS, J]], channel_multiplier=1).then_inc(prep_pool, 1)
            pool.wait_ge(prep_pool, 4)
            nc.gpsimd.affine_select(out=blockmask[:, :], in_=blockmask[:, :], compare_op=ALU.is_ge, fill=0.0,
                                    base=NS - 1, pattern=[[NS, J]], channel_multiplier=-1).then_inc(prep_pool, 1)
            pool.wait_ge(ids_in, 16)

            def gather(i, v):
                t = 2 * i + v
                if is_tile(i, 1):
                    for q in range(4):
                        pool.wait_ge(first_rows[v][q], 16 * min(8, NS - 8 * q))
                elif later(i):
                    pool.wait_ge(gathered[v], 16 * NS * (i - 1))
                nc.gpsimd.tensor_copy(idx[v][:, :], idx_all[:, bass.ds(t, 1), :].rearrange("p o n -> p (o n)"))\
                  .then_inc(idx_ready, 1)
                pool.wait_ge(idx_ready, t + 1)
                if later(2 * (t - 1)):
                    pool.wait_ge(scaled, 2 * (t - 1))
                pool.sem_inc(pool_step, 1)
                for n in range(NS):
                    pool.indirect_dma_start(
                        out=e_sb[v][:, n * D:(n + 1) * D], out_offset=None, in_=tables[n],
                        in_offset=bass.IndirectOffsetOnAxis(ap=idx[v][:, n:n + 1], axis=0))\
                        .then_inc(first_rows[v][n // 8] if is_tile(i, 0) else gathered[v], 16)

            for i in (0, 1):
                gather(i, 0)
                gather(i, 1)
            with pool.Fori(2, NT // 2) as i:
                gather(i, 0)
                gather(i, 1)

        @block.tensor
        def _(pe):
            mm = nc.tensor.matmul
            pe.wait_ge(w_early, W_EARLY)
            pe.wait_ge(consts_ready, 2)
            pe.wait_ge(prep_pool, 5)
            mm(pW[:, 0:D], avg[:, :], ws[:, :], start=True, stop=True).then_inc(prep_pe, 1)
            pe.wait_ge(prep_dve, 1)
            mm(pM[:, 0:128], ones[0:JN, :], mixw[:, :, :].rearrange("k j p -> k (j p)"), start=True, stop=True)\
                .then_inc(prep_pe, 1)
            pe.wait_ge(prep_dve, 2)
            wsc_flat = wsc2[:, :, :].rearrange("e a d -> e (a d)")
            mm(pZ[:, 0, 0:128], wsc_flat, wsc_flat, start=True, stop=True)
            nc.tensor.transpose(pZ[:, 2, 0:128], wscg2[:, :, :].rearrange("e a d -> e (a d)"), ident[:, :])\
              .then_inc(prep_pe, 1)
            pe.wait_ge(prep_dve, 3)
            for c in range(XC + 2):
                if c < XC:
                    pe.wait_ge(dt_in[2 * c // XC], 16)
                    for a in range(4):
                        t = 4 * c + a
                        for k in range(2):
                            last = mm(x_bank(c)[:, E * a:E * (a + 1)], dt_all[:, k, TB * t:TB * (t + 1)], wd[:, k, :],
                                      start=(k == 0), stop=(k == 1))
                    last.then_inc(x_raw, 1)
                if c >= 2:
                    pe.wait_ge(x_scaled, c - 1)
                    if c == 2:
                        pe.wait_ge(prep_dve, 4)
                    if c >= 4:
                        pe.wait_ge(x_out, c - 3)
                    for a in range(4):
                        last = nc.tensor.transpose(xt_bank(c)[:, TB * a:TB * (a + 1)], xr[:, c % 2, a, :], ident[:, :])
                    last.then_inc(x_tr, 1)

            pe.wait_ge(w_pairs, W_PAIRS)
            pe.wait_ge(late_dve, 1)
            pe.wait_ge(x_out, XC - 1)
            for k in range(5):
                last = mm(pM[:, 4 * k:4 * k + 4], selT_sb[:, 128 * k:128 * (k + 1)], gb[:, :], start=True, stop=True)
            last.then_inc(late_pe, 1)

            def late():
                pe.wait_ge(x_out, XC)
                for t in range(NT):
                    last = mm(pW[:, t:t + 1], x_all[:, TB * t:TB * (t + 1)], ones[:, 0:1], start=True, stop=True)
                last.then_inc(late_pe, 1)
                pe.wait_ge(w_late, W_LATE)
                pe.wait_ge(late_dve, 2)
                for k in range(5):
                    rows = 128 if k < 4 else K4
                    last = mm(pZ[0:K4, 0:2, :], dext[0:rows, k, :], wl[0:rows, k, :], start=(k == 0), stop=(k == 4))
                last.then_inc(late_pe, 1)

            def tile(i, u):
                t = 2 * i + u
                s = t + 1
                v = 1 - u

                def z_fill(c, f):
                    tz, c1 = (t, c - 1) if c else (t - 1, CH - 1)
                    if not exists(tz):
                        return
                    pe.wait_ge(t_ready, 8 * tz + 2 * c1 + f + 1)
                    if f == 0:
                        pe.wait_ge(xcol_ready, 4 * tz + c1 + 1)
                    if later(8 * tz + 2 * c1 + f):
                        pe.wait_ge(zs_ready, 2 * J * (8 * tz + 2 * c1 + f))
                    for a in range(4):
                        g = GC * c1 + 2 * a + f
                        last = mm(pZ[:, a, 0:TW], T[:, g, 0:JP], T[:, g, :], start=True, stop=True)
                    last.then_inc(z_full, 1)

                def ln1_transpose(s, w, si, q):
                    if not exists(s):
                        return
                    if is_tile(si, 0):
                        pe.wait_ge(first_rows[w][q], 16 * min(8, NS - 8 * q))
                    elif q == 0:
                        pe.wait_ge(gathered[w], 16 * NS * si)
                    if q < 2:
                        if later(4 * s):
                            pe.wait_ge(ege_ready, 4 * s)
                        else:
                            pe.wait_ge(x_scaled, XC)
                            pe.wait_ge(prep_dve, 4)
                        if later(s - 2):
                            pe.wait_ge(xt_rest, s - 2)
                    else:
                        pe.wait_ge(et_ready, 4 * s + q - 1)
                    for a in range(4 * q, min(4 * q + 4, NPAIR)):
                        last = nc.tensor.transpose(pA[:, q % 2, 128 * (a - 4 * q):128 * (a - 4 * q + 1)],
                                                   e_sb[w][:, 128 * a:128 * (a + 1)], ident[:, :])
                    last.then_inc(tr_full, 1)

                def ln1_gram(q):
                    if not exists(s):
                        return
                    if q < 2:
                        pe.wait_ge(et_ready, 4 * s + q + 3)
                    else:
                        pe.wait_ge(ege_ready, 4 * s + q - 1)
                    for a in range(4 * q, min(4 * q + 4, NPAIR)):
                        last = mm(pA[:, q % 2, 128 * (a - 4 * q):128 * (a - 4 * q + 1)], eT[:, a, :], gram[:, :],
                                  start=True, stop=True)
                    last.then_inc(gram_full, 1)

                def ln1_first(s, w):
                    for q in range(3):
                        ln1_transpose(s, w, 0, q)
                    ln1_gram(0)
                    ln1_transpose(s, w, 0, 3)
                    for q in range(1, 4):
                        ln1_gram(q)

                def mix(t, n, c, w, ti):
                    if not exists(t):
                        return
                    if c % 2 == 0:
                        pe.wait_ge(en_loaded[w][c // 2], 16 * (ti + 1))
                    if c == 0 and not later(t):
                        pe.wait_ge(late_dve, 3)
                    if later(2 * n):
                        pe.wait_ge(m_rest, 2 * n)
                    for k in range(4):
                        g = GC * c + 2 * k
                        last = mm(pM[:, 128 * k:128 * (k + 1)], en_sb[w][:, g:g + 2, :],
                                  mixw[:, :, :], start=True, stop=True)
                    last.then_inc(mix_full, 1)

                def project(c):
                    if not exists(t):
                        return
                    n = 4 * t + c
                    pe.wait_ge(m_ready, 2 * n + 2)
                    for h in range(2):
                        if later(2 * n + h - 1):
                            pe.wait_ge(t_ready, 2 * n + h - 1)
                        if h == 0:
                            rows, terms = D + 1, ((lhs0_hi, m0_hi), (lhs0_lo, m0_hi), (lhs0_hi, m0_lo))
                        else:
                            rows, terms = 128, ((lhs1_hi, m1_hi), (lhs1_lo, m1_hi), (lhs1_hi, m1_lo))
                        for a, (weights, m) in enumerate(terms):
                            if a == 2:
                                pe.wait_ge(m_rest, 2 * n + h + 1)
                            last = mm(pY[:, h, :], weights[0:rows, :], m[0:rows, :], start=(a == 0), stop=(a == 2))
                        last.then_inc(y_full, 1)

                def pairs():
                    if not exists(t - 1):
                        return
                    pe.wait_ge(cz_dve, 7 * t)
                    pe.wait_ge(cz_act, 2 * t)
                    if exists(s):
                        pe.wait_ge(ege_ready, 4 * (s + 1))
                    if u == 1 and exists(t - 3):
                        pe.wait_ge(h1_ready, 4 * (i - 1) + 3)
                    if u == 0 and exists(t - 4):
                        pe.wait_ge(h2_ready, 2 * (i - 1))
                    for k in range(5):
                        last = nc.tensor.transpose(pA[:, k // 4, 128 * (k % 4):128 * (k % 4 + 1)],
                                                   cz[:, 128 * k:128 * (k + 1)], ident[:, :])
                    last.then_inc(pair_full, 1)

                def wl_product(part):
                    if not exists(t - 1):
                        return
                    if part == WL_EARLY:
                        pe.wait_ge(xt_ready, t)
                        if is_tile(t, 1):
                            pe.wait_ge(wl_split, 3)
                        if u == 1 and exists(t - 3):
                            pe.wait_ge(h1_ready, 4 * (i - 1) + 3)
                        elif u == 0 and exists(t - 4):
                            pe.wait_ge(y_ready, i - 1)
                        elif exists(t - 2):
                            pe.wait_ge(hT_ready, 3 * (t - 1))
                    else:
                        pe.wait_ge(xt_rest, t)
                    for k, term in part:
                        rows = 128 if k < 4 else K4 if term else K4_REST + K4
                        x, w = ((xt_hi, wl_hi), (xt_hi, wl_lo), (xt_lo, wl_hi))[term]
                        first = part == WL_EARLY and (k, term) == (0, 0)
                        last = mm(pW[:, :], x[0:rows, k, :], w[0:rows, k, :],
                                  start=first, stop=(part == WL_LATE and (k, term) == (4, 0)))
                    if part == WL_LATE:
                        last.then_inc(out_full, 1)

                def z_transpose():
                    if not exists(t - 2):
                        return
                    pe.wait_ge(z_ready, t - 1)
                    if u == 0 and exists(t - 4):
                        pe.wait_ge(h1_ready, 4 * (i - 1))
                    for k in range(3):
                        last = nc.tensor.transpose(pW[:, 128 * k:128 * (k + 1)], z_sb[:, 128 * k:128 * (k + 1)],
                                                   ident[:, :])
                    last.then_inc(zt_full, 1)

                def mlp_first(m):
                    t0 = t - 3 if u == 1 else t - 4
                    if u != (m < 3) or not exists(t0) or is_tile(t0, NT - 2):
                        return
                    if m == 0:
                        pe.wait_ge(hT_ready, 3 * (t - 1))
                    elif m < 3:
                        if exists(s):
                            pe.wait_ge(ege_ready, 4 * (s + 1))
                    elif exists(t - 2):
                        pe.wait_ge(z_ready, t - 1)
                    else:
                        pe.wait_ge(h1_ready, 4 * (i - 2) + 1)
                    for k in range(5):
                        rhs = hT[:, k, :, :] if k < 3 else dt_all[:, k - 3, bass.ds(TB * t0, 2 * TB)]
                        last = mm(first_bank(m), w1[:, k, 128 * m:128 * (m + 1)], rhs,
                                  start=(k == 0), stop=(k == 4))
                    last.then_inc(h1_full, 1)

                def last_first(part):
                    pe.wait_ge(hT_ready, 3 * (NT - 1))
                    pe.wait_ge(t_ready, 8 * NT)
                    pe.wait_ge(zs_ready, 16 * J * NT)
                    for m in part:
                        for k in (3, 4):
                            mm(last_bank(m), w1[:, k, 128 * m:128 * (m + 1)], dt_all[:, k - 3, TB * (NT - 2):B],
                               start=(k == 3), stop=False)
                        for k in range(3):
                            mm(last_bank(m)[:, 0:TB], w1[:, k, 128 * m:128 * (m + 1)], hT[:, k, 0, :],
                               start=False, stop=False)

                def last_rest():
                    pe.wait_ge(hT_ready, 3 * NT)
                    for m in range(4):
                        for k in range(3):
                            last = mm(last_bank(m)[:, TB:2 * TB], w1[:, k, 128 * m:128 * (m + 1)], hT[:, k, 1, :],
                                      start=False, stop=(k == 2))
                        last.then_inc(h1_full, 1)

                def mlp_second(m, part):
                    if not (u == 0 and exists(t - 4)):
                        return
                    pe.wait_ge(h1_ready, 4 * (i - 1))
                    if exists(s):
                        pe.wait_ge(ege_ready, 4 * (s + 1))
                    for k in part:
                        last = mm(pA[:, m, 0:2 * TB], w2[:, k, 128 * m:128 * (m + 1)], h1T[:, k, :],
                                  start=(k == 0), stop=(k == 3))
                    if 3 in part:
                        last.then_inc(h2_full, 1)

                def mlp_third():
                    if not (u == 0 and exists(t - 4)):
                        return
                    pe.wait_ge(h2_ready, 2 * (i - 1))
                    if exists(t - 2):
                        pe.wait_ge(hT_ready, 3 * (t - 1))
                    for k in range(2):
                        last = mm(pW[0:1, 0:256], w3[:, k:k + 1], h2T[:, k, :], start=(k == 0), stop=(k == 1))
                    last.then_inc(top_full, 1)

                if is_tile(t, -1):
                    ln1_first(0, 0)
                if is_tile(t, 0):
                    mix(0, 0, 0, 0, 0)
                for c in range(CH):
                    n = 4 * t + c
                    z_fill(c, 0)
                    if c == 3:
                        pairs()
                    project(c)
                    if c == 0 and is_tile(t, 0):
                        mix(0, 1, 1, 0, 0)
                        ln1_first(1, 1)
                    elif c == 0 and later(t + 1):
                        ln1_gram(0)
                        ln1_gram(1)
                    if c == 1 and is_tile(t, NT + 1):
                        last_rest()
                    if c == 1:
                        mlp_first(0)
                        mlp_first(3)
                    if c == 2:
                        mlp_second(0, (2, 3))
                    if c == 3:
                        mlp_third()
                        if u == 1:
                            wl_product(WL_EARLY)
                        if later(t + 1):
                            ln1_transpose(t + 2, u, i + 1, 0)
                            ln1_transpose(t + 2, u, i + 1, 1)
                        if u == 0:
                            wl_product(WL_EARLY)
                    if c < 3 and not (c == 0 and is_tile(t, 0)):
                        mix(t, n + 1, c + 1, u, i)
                    if c == 3 and not is_tile(s, 0):
                        mix(s, n + 1, 0, v, i + u)
                    z_fill(c, 1)
                    if c == 0 and later(t):
                        ln1_gram(2)
                        ln1_gram(3)
                    if c == 0 and u == 1:
                        z_transpose()
                    if c == 1:
                        if u == 0:
                            z_transpose()
                        mlp_first(1)
                        mlp_second(0, (0, 1))
                    if c == 2:
                        mlp_first(2)
                        mlp_second(1, (0, 1, 2, 3))
                        if is_tile(t, NT):
                            last_first((0,))
                    if c == 3:
                        wl_product(WL_LATE)
                        if is_tile(t, NT):
                            last_first((1, 2, 3))
                        if later(t + 1):
                            ln1_transpose(t + 2, u, i + 1, 2)
                            ln1_transpose(t + 2, u, i + 1, 3)

            tiles(pe, tile, late)

        @block.scalar
        def _(act):
            def copy(out, in_, **k):
                return nc.scalar.activation(out, in_, ACT.Copy, **k)

            act.wait_ge(w_dense, W_DENSE)
            act.wait_ge(consts_ready, 2)
            for c in range(XC + 1):
                if c < XC:
                    act.wait_ge(x_raw, c + 1)
                    if c >= 2:
                        act.wait_ge(x_ssq, c - 1)
                    nc.scalar.activation(xsq[:, c % 2, :, :].rearrange("b a e -> b (a e)"), x_bank(c), ACT.Square)\
                        .then_inc(x_sq, 1)
                    act.wait_ge(x_ssq, c + 1)
                    nc.scalar.activation(xsd[:, 4 * c:4 * c + 4], xss[:, 4 * c:4 * c + 4], ACT.Sqrt,
                                         bias=eps[:, 0:1], scale=1.0 / E).then_inc(x_sd, 1)
                if c >= 1:
                    act.wait_ge(x_tr, c)
                    nc.scalar.activation(x_all[:, 512 * (c - 1):512 * c], xt_bank(c - 1)[:, :], ACT.Identity,
                                         bias=vecs[:, 1:2], scale=vecs[:, 0:1]).then_inc(x_out, 1)

            def tile(i, u):
                t = 2 * i + u
                s = t + 1
                v = 1 - u

                def z_copy(c, f):
                    tz, c1, w = (t, c - 1, u) if c else (t - 1, CH - 1, v)
                    if not exists(tz):
                        return
                    if c1 == 0 and f == 0 and later(32 * i):
                        act.wait_ge(zs_stored[w], 32 * i)
                    act.wait_ge(z_full, 8 * tz + 2 * c1 + f + 1)
                    groups = slice(GC * c1 + f, GC * (c1 + 1), 2)
                    for j in range(J):
                        quad = slice(P * j, P * (j + 1))
                        copy(zs[w][quad, groups, 0:P], pZ[quad, :, quad]).then_inc(zs_ready, 1)
                        copy(zs[w][quad, groups, P:W34], pZ[quad, :, JP + j:TW:J]).then_inc(zs_ready, 1)

                def ln1_copy(s, q):
                    if not exists(s):
                        return
                    act.wait_ge(tr_full, 4 * s + q + 1)
                    if q == 0 and later(4 * s):
                        act.wait_ge(gram_full, 4 * s)
                    a, n = 4 * q, min(4, NPAIR - 4 * q)
                    copy(eT[:, a:a + n, :], pA[:, q % 2, 0:128 * n]).then_inc(et_ready, 1)

                def ln1_sqrt():
                    if not exists(s):
                        return
                    act.wait_ge(var1_ready, 4 * s + 3)
                    nc.scalar.activation(sd1[:, :], var1[:, :], ACT.Sqrt, bias=eps[:, 0:1]).then_inc(sd1_ready, 1)

                def mixed(t, n, c):
                    if not exists(t):
                        return
                    act.wait_ge(mix_full, n + 1)
                    if later(2 * n):
                        act.wait_ge(y_full, 2 * n)
                    copy(m0_hi[0:D, :], pM[0:D, :]).then_inc(m_ready, 1)
                    copy(m1_hi[D:128, :], pM[D:128, :]).then_inc(m_ready, 1)

                def x_columns(t, c):
                    if not exists(t):
                        return
                    if later(8 * t + 2 * c - 6):
                        act.wait_ge(z_full, 8 * t + 2 * c - 6)
                    copy(T[:, GC * c:GC * (c + 1), JP:JP + J],
                         x_all[:, bass.ds(TB * t + 32 * c, 32)].rearrange("e (g j) -> e g j", j=J))\
                        .then_inc(xcol_ready, 1)

                def z_features():
                    if not exists(t - 2):
                        return
                    act.wait_ge(zt_full, t - 1)
                    if later(4 * (i - 1)):
                        act.wait_ge(h1_full, 4 * (i - 1))
                    for k in range(3):
                        nc.scalar.activation(hT[:, k, u, :], pW[:, 128 * k:128 * (k + 1)], ACT.Identity,
                                             bias=bl_sb[:, k:k + 1], scale=gl_sb[:, k:k + 1]).then_inc(hT_ready, 1)

                def ln3_sqrt(t):
                    if not exists(t - 1):
                        return
                    act.wait_ge(ln3_ready, 2 * t - 1)
                    nc.scalar.activation(sd3[:, :], mv[:, 1:2], ACT.Sqrt, bias=eps[:, 0:1]).then_inc(sd3_ready, 1)

                def relu_first(m):
                    if not is_tile(t, NT + 1) and u != (m < 3) or not exists(t - 3 if u == 1 else t - 4):
                        return
                    act.wait_ge(h1_full, 4 * (i - 1) + m + 1 if u == 1 else 4 * (i - 1))
                    if m == 0 and later(2 * (i - 1)):
                        act.wait_ge(h2_full, 2 * (i - 1))
                    bank = last_bank(m) if is_tile(t, NT + 1) else first_bank(m)
                    nc.scalar.activation(h1T[:, m, :], bank, ACT.Relu,
                                         bias=b1[:, m:m + 1]).then_inc(h1_ready, 1)

                def relu_second(m):
                    if not (u == 0 and exists(t - 4)):
                        return
                    act.wait_ge(h2_full, 2 * (i - 2) + m + 1)
                    if m == 0 and later(i - 2):
                        act.wait_ge(top_full, i - 2)
                    nc.scalar.activation(h2T[:, m, :], pA[:, m, 0:2 * TB], ACT.Relu,
                                         bias=b2[:, m:m + 1]).then_inc(h2_ready, 1)

                if is_tile(t, -1):
                    for q in range(4):
                        ln1_copy(0, q)
                if is_tile(t, 0):
                    mixed(0, 0, 0)
                    x_columns(0, 0)
                for c in range(CH):
                    n = 4 * t + c
                    if c == 3 and exists(t - 1):
                        act.wait_ge(pair_full, t)
                        if later(t - 1):
                            act.wait_ge(out_full, t - 1)
                        copy(xt_hi[:, :, :].rearrange("p k b -> p (k b)"),
                             pA[:, :, :].rearrange("p h b -> p (h b)")[:, 0:5 * TB]).then_inc(xt_ready, 1)
                    early = c == 2 and u == 1
                    if early:
                        z_copy(c, 0)
                    if exists(t):
                        for h in range(2):
                            act.wait_ge(y_full, 2 * n + h + 1)
                            if later(2 * n + h - 1):
                                act.wait_ge(ssq_ready, 2 * n + h - 1)
                            nc.scalar.activation(sq[:, h, :], pY[:, h, :], ACT.Square).then_inc(sq_ready, 1)
                    if c == 3 and u == 0 and exists(t - 4):
                        act.wait_ge(top_full, i - 1)
                        copy(y_sb[:, bass.ds(TB * (t - 4), 2 * TB)], pW[0:1, 0:256]).then_inc(y_ready, 1)
                    if not early:
                        z_copy(c, 0)
                    if c == 2 and exists(t - 1):
                        act.wait_ge(zb_loaded[v], 16 * (i + u))
                        if later(t - 1):
                            act.wait_ge(pair_full, t - 1)
                        copy(cz[:, 0:256].rearrange("b (r c) -> b r c", c=16), zb[v][:, 16:32, 0:16])\
                            .then_inc(cz_act, 1)
                        copy(cz[:, 256:384].rearrange("b (s r c) -> b s r c", r=8, c=8), rects(v, 8))\
                            .then_inc(cz_act, 1)
                    if exists(t):
                        for h in range(2):
                            act.wait_ge(ssq_ready, 2 * n + h + 1)
                            if later(2 * n + h - 1):
                                act.wait_ge(rstd2_ready, 2 * n + h - 1)
                            nc.scalar.activation(sd2[:, h, :], ssq[:, h, :], ACT.Sqrt, bias=eps[:, 1:2])\
                                .then_inc(sd2_ready, 1)
                    if c == 0 and is_tile(t, 0):
                        mixed(0, 1, 1)
                        for q in range(4):
                            ln1_copy(1, q)
                    if c == 1:
                        for m in range(4) if is_tile(t, NT + 1) else (0, 3):
                            if not is_tile(t, NT + 2):
                                relu_first(m)
                    if c == 3 and later(t + 1):
                        ln1_copy(t + 2, 0)
                        ln1_copy(t + 2, 1)
                    if c < 3 and not (c == 0 and is_tile(t, 0)):
                        mixed(t, n + 1, c + 1)
                    if c == 3 and not is_tile(s, 0):
                        mixed(s, n + 1, 0)
                    if c == 1 and u == 1:
                        ln1_sqrt()
                    z_copy(c, 1)
                    if c == 1 and u == 0 and not is_tile(t, 0):
                        ln1_sqrt()
                    if c == 3 and not is_tile(t, NT - 1):
                        ln3_sqrt(t)
                    if c == 0 and is_tile(t, NT):
                        ln3_sqrt(t - 1)
                    if c == 0 and is_tile(t, 0):
                        ln1_sqrt()
                    if c == 0 and u == 1:
                        z_features()
                    if c < 3:
                        x_columns(t, c + 1)
                    elif not is_tile(s, 0):
                        x_columns(s, 0)
                    if c == 1:
                        if u == 0:
                            z_features()
                        if not is_tile(t, NT + 1):
                            relu_first(1)
                    if c == 2:
                        if not is_tile(t, NT + 1):
                            relu_first(2)
                        relu_second(0)
                        relu_second(1)
                    if c == 3 and later(t + 1):
                        ln1_copy(t + 2, 2)
                        ln1_copy(t + 2, 3)

            def late():
                act.wait_ge(w_late, W_LATE)

            tiles(act, tile, late)

        @block.vector
        def _(dve):
            V = nc.vector
            chain = [0]

            def link(ins):
                chain[0] += 1
                ins.then_inc(consts_chain, 1)
                dve.wait_ge(consts_chain, chain[0])

            V.memset(lhs1[0:D, :], 0.0)
            V.memset(gb[:, :], 0.0)
            link(V.memset(wl[0:64, 4, :], 0.0))
            V.memset(eps[:, 0:1], EPS).then_inc(consts_ready, 1)
            V.memset(ones[:, :], 1.0)
            V.memset(gram[:, :], 0.0)
            V.memset(eps[:, 1:2], P * EPS)
            link(V.memset(cz[:, 512:640], 0.0))
            V.memset(avg[:, :], 1.0 / E).then_inc(consts_ready, 1)
            dve.wait_ge(w_early, W_EARLY)
            dve.wait_ge(prep_pool, 5)
            link(V.tensor_reduce(wsisum[:, :], wsi4[:, :], X, ALU.add))
            link(V.tensor_scalar(wsisum[:, :], wsisum[:, :], -1.0 / P, None, ALU.mult))
            link(V.tensor_scalar(wsi4[:, :], wsi4[:, :], wsisum[:, 0:1], None, ALU.add))
            for j in range(J):
                ins = V.tensor_scalar(mixw[:, j, :], wsi4[:, :], blockmask[:, j:j + 1], None, ALU.mult)
            ins.then_inc(prep_dve, 1)
            dve.wait_ge(prep_pe, 1)
            V.tensor_tensor(wsc2[:, 0, :], ws[:, :], pW[:, 0:D], ALU.subtract)
            link(V.tensor_tensor(wsc2[:, 1, :], ws[:, :], pW[:, 0:D], ALU.subtract))
            V.tensor_scalar(wscg2[:, :, :], wsc2[:, :, :], vecs[:, 2:3], None, ALU.mult).then_inc(prep_dve, 1)
            dve.wait_ge(w_dense, W_DENSE)
            link(V.tensor_reduce(wdsum[:, :], wd[:, :, :], X, ALU.add))
            link(V.tensor_scalar(wdsum[:, :], wdsum[:, :], -1.0 / E, None, ALU.mult))
            V.tensor_scalar(wd[:, 0, :], wd[:, 0, :], wdsum[:, 0:1], None, ALU.add)
            V.tensor_scalar(wd[:, 1, :], wd[:, 1, :], wdsum[:, 1:2], None, ALU.add).then_inc(prep_dve, 1)
            dve.wait_ge(prep_pe, 3)
            for h in range(2):
                q = slice(D * h, D * (h + 1))
                V.tensor_scalar(gram[q, q], pZ[q, 0, q], 1.0 / E, None, ALU.mult)
            V.tensor_copy(lhs0[0:D, :], pZ[0:D, 2, 0:128])
            V.tensor_copy(lhs1[D:128, :], pZ[D:128, 2, 0:128])
            V.memset(m1_rows[:, :], 0.0)
            link(V.memset(T[:, :, JP + J:TW], 1.0))
            link(V.tensor_copy(m1_rows[0:1, :], pM[0:1, 0:128]))
            bias_row = pM[D:D + 1, 0:128].unsqueeze(1).to_broadcast([1, 4, 128])
            upper_rows = m1_rows[:, :].unsqueeze(1).to_broadcast([D, 4, 128])
            by_group = "d (r c) -> d r c"
            V.tensor_copy(m0_hi[D:D + 1, :].rearrange(by_group, c=128), bias_row)
            V.tensor_copy(m1_hi[0:D, :].rearrange(by_group, c=128), upper_rows)
            V.tensor_copy(lhs0_hi[0:D + 1, :], lhs0[0:D + 1, :])
            link(V.tensor_copy(lhs1_hi[:, :], lhs1[:, :]))
            V.tensor_tensor(m0_lo[D:D + 1, :].rearrange(by_group, c=128), bias_row,
                            m0_hi[D:D + 1, :].rearrange(by_group, c=128), ALU.subtract)
            V.tensor_tensor(m1_lo[0:D, :].rearrange(by_group, c=128), upper_rows,
                            m1_hi[0:D, :].rearrange(by_group, c=128), ALU.subtract)
            V.tensor_tensor(lhs0_lo[0:D + 1, :], lhs0[0:D + 1, :], lhs0_hi[0:D + 1, :], ALU.subtract)
            V.tensor_tensor(lhs1_lo[:, :], lhs1[:, :], lhs1_hi[:, :], ALU.subtract).then_inc(prep_dve, 1)
            for c in range(XC):
                dve.wait_ge(x_sq, c + 1)
                V.tensor_reduce(xss[:, 4 * c:4 * c + 4], xsq[:, c % 2, :, :], X, ALU.add).then_inc(x_ssq, 1)
                dve.wait_ge(x_sd, c + 1)
                V.reciprocal(xrstd[:, 4 * c:4 * c + 4], xsd[:, 4 * c:4 * c + 4]).then_inc(x_rstd, 1)
                dve.wait_ge(x_rstd, c + 1)
                if c >= 2:
                    dve.wait_ge(x_tr, c - 1)
                V.tensor_tensor(xr[:, c % 2, :, :], x_bank(c).rearrange("b (a e) -> b a e", e=E),
                                xrstd[:, 4 * c:4 * c + 4].unsqueeze(2).to_broadcast([TB, 4, E]), ALU.mult)\
                    .then_inc(x_scaled, 1)
            dve.wait_ge(w_pairs, W_PAIRS)
            V.tensor_scalar(gb[:, 0:4:2], gb[:, 0:4:2], float(P) ** 0.5, None, ALU.mult).then_inc(late_dve, 1)
            link(V.memset(dext[:, :, :], 0.0))
            V.memset(cz[:, 512 + P + 1:512 + P + 2], 1.0)
            dve.wait_ge(late_pe, 1)
            link(V.tensor_copy(pv[:, :, :], pM[:, 0:20].rearrange("p (k a) -> p k a", a=4)))
            gp, bp, gq, bq = (pv[:, :, a] for a in range(4))
            V.tensor_tensor(pg[:, 3, :], gq, isx_sb[:, :], ALU.add)
            V.tensor_tensor(pg[:, 1, :], gp, bq, ALU.mult)
            link(V.tensor_tensor(pg[:, 2, :], gq, bp, ALU.mult))
            V.tensor_tensor(pg[:, 0, :], gp, pg[:, 3, :], ALU.mult)
            V.tensor_tensor(dext[:, :, P], isx_sb[:, :], bp, ALU.mult)
            V.scalar_tensor_tensor(dext[:, :, P + 1], bp, float(E), bq, ALU.mult, ALU.mult)
            for k in range(5):
                ins = V.tensor_scalar(dtmp[:, k, :], sel_sb[:, 0, k, :], pg[:, 1, k:k + 1], None, ALU.mult)
            link(ins)
            for k in range(5):
                ins = V.scalar_tensor_tensor(dext[:, k, 0:P], sel_sb[:, 1, k, :], pg[:, 2, k:k + 1],
                                             dtmp[:, k, :], ALU.mult, ALU.add)
            ins.then_inc(late_dve, 1)

            def late():
                dve.wait_ge(late_pe, 2)
                V.tensor_copy(sx_all[:, :], pW[:, 0:NT])
                dve.wait_ge(late_pe, 3)
                for k in range(4):
                    V.tensor_scalar(wl[:, k, :], wl[:, k, :], pg[:, 0, k:k + 1], None, ALU.mult)
                V.scalar_tensor_tensor(wl[0:K4, 4, :], wl[0:K4, 4, :], pg[0:K4, 0, 4:5],
                                       pZ[0:K4, 0:2, :].rearrange("p a m -> p (a m)"), ALU.mult, ALU.add)\
                    .then_inc(late_dve, 1)

            def tile(i, u):
                t = 2 * i + u
                s = t + 1
                v = 1 - u

                def ln1_product(q):
                    if not exists(s):
                        return
                    if is_tile(i + u, 0):
                        dve.wait_ge(first_rows[v][q], 16 * min(8, NS - 8 * q))
                    elif q == 0:
                        dve.wait_ge(gathered[v], 16 * NS * (i + u))
                    dve.wait_ge(gram_full, 4 * s + q + 1)
                    a, n = 512 * q, min(512, NS * D - 512 * q)
                    flat = ege[:, :, :].rearrange("b n d -> b (n d)")
                    V.tensor_tensor(flat[:, a:a + n], pA[:, q % 2, 0:n], e_sb[v][:, a:a + n], ALU.mult)\
                        .then_inc(ege_ready, 1)

                def ln1_sum(h):
                    if not exists(s):
                        return
                    half = slice(NS // 2 * h, NS // 2 * (h + 1))
                    dve.wait_ge(ege_ready, 4 * s + 2 * (h + 1))
                    V.tensor_reduce(var1[:, half], ege[:, half, :], X, ALU.add).then_inc(var1_ready, 1)

                def ln1_guard():
                    if not exists(s):
                        return
                    dve.wait_ge(var1_ready, 4 * s + 2)
                    V.tensor_scalar(var1[:, :], var1[:, :], 0.0, None, ALU.max).then_inc(var1_ready, 1)

                def ln1_scale(h):
                    if not exists(s):
                        return
                    if h == 0:
                        dve.wait_ge(sd1_ready, s + 1)
                        V.reciprocal(rstd1[:, :], sd1[:, :]).then_inc(var1_ready, 1)
                        dve.wait_ge(var1_ready, 4 * s + 4)
                        if later(32 * (i + 1)):
                            dve.wait_ge(es_stored[u], 32 * (i + 1))
                    half = slice(NS // 2 * h, NS // 2 * (h + 1))
                    V.tensor_tensor(es_sb[:, half, :],
                                    e_sb[v][:, :].rearrange("b (n d) -> b n d", d=D)[:, half, :],
                                    rstd1[:, half].unsqueeze(2).to_broadcast([TB, NS // 2, D]), ALU.mult)\
                        .then_inc(scaled, 1)

                def ln1_at_once():
                    for h in range(2):
                        ln1_product(2 * h)
                        ln1_product(2 * h + 1)
                        ln1_sum(h)
                    ln1_guard()
                    ln1_scale(0)
                    ln1_scale(1)

                def compact():
                    if not exists(t - 1):
                        return
                    dve.wait_ge(zb_loaded[v], 16 * (i + u))
                    if later(t - 1):
                        dve.wait_ge(pair_full, t - 1)
                    V.tensor_copy(cz[:, 384:448].rearrange("b (s r c) -> b s r c", r=4, c=4), rects(v, 4))\
                        .then_inc(cz_dve, 1)
                    V.tensor_copy(cz[:, 448:480].rearrange("b (s r c) -> b s r c", r=2, c=2), rects(v, 2))\
                        .then_inc(cz_dve, 1)
                    V.tensor_copy(cz[:, 480:496], rects(v, 1)).then_inc(cz_dve, 1)
                    V.tensor_copy(cz[:, 496:512], zb[v][:, 0:16, P]).then_inc(cz_dve, 1)
                    V.tensor_copy(cz[:, 512 + N_EXT:512 + K4], zb[v][:, 16:32, P]).then_inc(cz_dve, 1)
                    V.tensor_copy(cz[:, 512:512 + P], zb[v][:, :, P + 1]).then_inc(cz_dve, 1)
                    V.tensor_copy(cz[:, 512 + P:512 + P + 1], sx_all[:, bass.ds(t - 1, 1)]).then_inc(cz_dve, 1)

                def pairs_rest():
                    if not exists(t - 1):
                        return
                    dve.wait_ge(xt_ready, t)
                    if later(t - 1):
                        dve.wait_ge(out_full, t - 1)
                    V.tensor_tensor(xt_lo[:, :, :].rearrange("p k b -> p (k b)"), pA[:, 0, :],
                                    xt_hi[:, 0:4, :].rearrange("p k b -> p (k b)"), ALU.subtract)
                    V.tensor_tensor(xt_hi[K4_REST:K4_REST + K4, 4, :], pA[0:K4, 1, 0:TB], xt_hi[0:K4, 4, :],
                                    ALU.subtract).then_inc(xt_rest, 1)

                def ln3_statistics(t):
                    if not exists(t - 1):
                        return
                    dve.wait_ge(out_full, t)
                    V.bn_stats(bn6[:, :], pW[:, :]).then_inc(bn_ready, 1)
                    dve.wait_ge(bn_ready, t)
                    dve.sem_inc(dve_step, 1)
                    V.bn_aggr(mv[:, :], bn6[:, :]).then_inc(ln3_ready, 1)

                def ln3_rows(t):
                    if not exists(t - 1):
                        return
                    dve.wait_ge(sd3_ready, t)
                    V.reciprocal(rstd3[:, :], sd3[:, :]).then_inc(ln3_ready, 1)
                    dve.wait_ge(ln3_ready, 2 * t)
                    if later(t - 1):
                        dve.wait_ge(zt_full, t - 1)
                    V.tensor_scalar(z_sb[:, :], pW[:, 0:DIMS], mv[:, 0:1], rstd3[:, 0:1], ALU.subtract, ALU.mult)\
                        .then_inc(z_ready, 1)

                def sum_squares(n, h):
                    if not exists(t):
                        return
                    dve.wait_ge(sq_ready, 2 * n + h + 1)
                    V.tensor_reduce(ssq[:, h, :], sq[:, h, :].rearrange("e (b p) -> e b p", p=P), X, ALU.add)\
                        .then_inc(ssq_ready, 1)

                def normalize(c, n, h):
                    if not exists(t):
                        return
                    dve.wait_ge(sd2_ready, 2 * n + h + 1)
                    V.reciprocal(rstd2[:, h, :], sd2[:, h, :]).then_inc(rstd2_ready, 1)
                    dve.wait_ge(rstd2_ready, 2 * n + h + 1)
                    if later(8 * t + 2 * c + h - 7):
                        dve.wait_ge(z_full, 8 * t + 2 * c + h - 7)
                    V.tensor_tensor(T[:, GC * c + h:GC * (c + 1):2, 0:JP].rearrange("e k (j p) -> e k j p", p=P),
                                    pY[:, h, :].rearrange("e (k j p) -> e k j p", j=J, p=P),
                                    rstd2[:, h, :].rearrange("e (k j) -> e k j", j=J).unsqueeze(3)
                                    .to_broadcast([E, 4, J, P]), ALU.mult).then_inc(t_ready, 1)

                if is_tile(t, -1):
                    ln1_at_once()
                def mixed_rest(t, n):
                    if not exists(t):
                        return
                    dve.wait_ge(m_ready, 2 * n + 1)
                    if later(2 * n):
                        dve.wait_ge(y_full, 2 * n)
                    V.tensor_tensor(m0_lo[0:D, :], pM[0:D, :], m0_hi[0:D, :], ALU.subtract).then_inc(m_rest, 1)
                    dve.wait_ge(m_ready, 2 * n + 2)
                    V.tensor_tensor(m1_lo[D:128, :], pM[D:128, :], m1_hi[D:128, :], ALU.subtract).then_inc(m_rest, 1)

                def split_wl(blocks):
                    for k in blocks:
                        rows = 128 if k < 4 else K4
                        if k == 4:
                            rows = K4_REST
                            V.tensor_copy(wl_hi[K4_REST:K4_REST + K4, k, :], wl[0:K4, k, :])
                        ins = V.tensor_copy(wl_hi[0:rows, k, :], wl[0:rows, k, :])
                    link(ins)
                    for k in blocks:
                        rows = 128 if k < 4 else K4
                        ins = V.tensor_tensor(wl_lo[0:rows, k, :], wl[0:rows, k, :], wl_hi[0:rows, k, :], ALU.subtract)
                    ins.then_inc(wl_split, 1)

                if is_tile(t, 0):
                    mixed_rest(0, 0)
                for c in range(CH):
                    n = 4 * t + c
                    if c == 2 and later(t):
                        ln1_scale(1)
                    if c == 3:
                        pairs_rest()
                    sum_squares(n, 0)
                    sum_squares(n, 1)
                    normalize(c, n, 0)
                    if c == 0 and is_tile(t, 0):
                        normalize(0, 0, 1)
                        mixed_rest(0, 1)
                        ln1_at_once()
                    elif c == 0 and later(t + 1):
                        ln1_product(0)
                        ln1_product(1)
                        mixed_rest(t, n + 1)
                        normalize(0, n, 1)
                        ln1_product(2)
                        ln1_product(3)
                        ln1_sum(0)
                        if is_tile(t, NT):
                            ln3_statistics(t - 1)
                            ln3_rows(t - 1)
                    if c == 1:
                        if later(t):
                            ln1_sum(1)
                            ln1_guard()
                        normalize(1, n, 1)
                        mixed_rest(t, n + 1)
                        if later(t):
                            ln1_scale(0)
                    if c == 2:
                        compact()
                        mixed_rest(t, n + 1)
                        normalize(2, n, 1)
                    if c == 3:
                        normalize(3, n, 1)
                        if not is_tile(s, 0):
                            mixed_rest(s, n + 1)
                        if not is_tile(t, NT - 1):
                            ln3_statistics(t)
                            ln3_rows(t)
                    if c > 0 and is_tile(t, 0):
                        split_wl(((0, 1), (2, 3), (4,))[c - 1])

            tiles(dve, tile, late)


def kernel(**inputs):
    import concourse.bacc as bacc
    from concourse.bass_utils import run_bass_kernel_spmd as run

    nc = bacc.Bacc("TRN2", target_bir_lowering=False, num_devices=1)
    blocks = pair_blocks()
    f32 = np.float32
    selT = np.zeros((2 * P, 5 * 128), f32)
    sel = np.zeros((128, 2, 5, P), f32)
    isx = np.zeros((128, 5), f32)
    columns = []
    for k, rows in enumerate(blocks):
        for r, pair in enumerate(rows):
            if pair is None:
                continue
            p, q = pair
            columns.append(p * (p + 1) // 2 + q + 1)
            for h, c in ((0, p), (1, q)):
                if c >= 0:
                    selT[P * h + c, 128 * k + r] = 1
                    sel[r, h, k, c] = 1
            isx[r, k] = q < 0
    a = {k: np.asarray(v) for k, v in inputs.items()}
    col = lambda x: x.reshape(-1, 1)
    blocked = lambda x: np.ascontiguousarray(x.reshape(-1, 128).T)
    arrays = {
        "ids": a["ids"],
        **{f"tbl_{n}": a[f"tbl_{n}"] for n in range(NS)},
        "dT": a["r_dense_t"].T, "WdT": a["L0_rec_Wd"].T, "gd": col(a["L0_rec_gd"]), "bd": col(a["L0_rec_bd"]),
        "Ws": a["L0_rec_Ws"], "gs": col(a["L0_rec_gs"]), "bs": a["L0_rec_bs"].reshape(1, -1),
        "WsiT": a["L0_rec_Wsi"].T, "gsi": col(a["L0_rec_gsi"]), "bsi": col(a["L0_rec_bsi"]),
        "WlT": a["L0_rec_Wl"].T[columns], "glc": blocked(a["L0_rec_gl"][:DIMS]),
        "blc": blocked(a["L0_rec_bl"][:DIMS]),
        "W1": a["W_top1"], "b1c": blocked(a["b_top1"]), "W2": a["W_top2"], "b2c": blocked(a["b_top2"]),
        "W3c": blocked(a["W_top3"]), "selT": selT, "sel": sel, "isx": isx,
    }
    arrays = {k: np.ascontiguousarray(v) for k, v in arrays.items()}
    aps = {k: nc.dram_tensor(k, v.shape, mybir.dt.from_np(v.dtype), kind="ExternalInput").ap()
           for k, v in arrays.items()}
    tables = [aps.pop(f"tbl_{n}") for n in range(NS)]
    y = nc.dram_tensor("y", (B, 1), mybir.dt.float32, kind="ExternalOutput").ap()
    e_dram = nc.dram_tensor("e_dram", (NT, TB * NS, D), mybir.dt.float32, kind="Internal").ap()
    z_dram = nc.dram_tensor("z_dram", (NT, G, J, P, W34), mybir.dt.float32, kind="Internal").ap()
    build(nc, tables=tables, y_out=y, e_dram=e_dram, z_dram=z_dram, **aps)
    r = run(nc, [arrays], core_ids=[0])
    return r.results[0]["y"]
```
